# Optimizing a Trainium2 kernel written in Bass

```python
import numpy as np
import jax
import jax.numpy as jnp

def _softmax(x, axis=-1):
    return jax.nn.softmax(x, axis=axis)

def _gelu(x):
    return jax.nn.gelu(x, approximate=True)

def _silu(x):
    return jax.nn.silu(x)

def _sigmoid(x):
    return jax.nn.sigmoid(x)

def _layernorm(x, axis=-1, eps=1e-05):
    m = jnp.mean(x, axis=axis, keepdims=True)
    v = jnp.var(x, axis=axis, keepdims=True)
    return (x - m) / jnp.sqrt(v + eps)

def _scatter_add(tgt, idx, src, axis=0):
    return tgt.at[idx].add(src)

def _segment_sum(src, seg, n):
    return jax.ops.segment_sum(src, seg, n)
kernel_name = 'mk_adj_ffn_d1_adj_r2_c44228'

def setup_inputs(seed: int=0):
    np.random.seed(seed)
    _w = jnp.asarray

    def _rec_inputs():
        import jax
        import jax.numpy as jnp
        _gk = jax.random.key(seed)
        x = -0.0001546 + 1 * jax.random.normal(jax.random.fold_in(_gk, 1), (128, 128, 128), jnp.float32)
        _a = jax.random.bernoulli(jax.random.fold_in(_gk, 2), 0.125, (128, 128))
        _a = jnp.logical_or(_a, jnp.swapaxes(_a, -1, -2))
        _a = jnp.logical_or(_a, jnp.eye(128, dtype=bool))
        _af = _a.astype(jnp.float32)
        _af = _af * jax.random.uniform(jax.random.fold_in(_gk, 3), (128, 128), jnp.float32, 0.05, 0.999927)
        adj = _af
        return (x, adj)
    x, adj = _rec_inputs()

    def _L0_gnn_setup():
        import jax, jax.numpy as jnp
        import numpy as np
        B, N, D = (2048, 128, 128)
        key = jax.random.key(seed)
        ks = jax.random.split(key, 6)
        return {'label': jax.random.normal(ks[0], (B, N, D), dtype=jnp.float32), 'adj_in': jax.random.uniform(ks[1], (N, N), dtype=jnp.float32), 'adj_out': jax.random.uniform(ks[2], (N, N), dtype=jnp.float32), 'edge_bias': jnp.zeros((N, D), dtype=jnp.float32), 'gate_weight': jax.random.normal(ks[3], (D, 1), dtype=jnp.float32) * (6.0 / (D + 1)) ** 0.5, 'bias_gate': jnp.zeros((N, 1), dtype=jnp.float32), 'out_edge_bias': jnp.zeros((N, D), dtype=jnp.float32), 'out_gate_weight': jax.random.normal(ks[4], (D, 1), dtype=jnp.float32) * (6.0 / (D + 1)) ** 0.5, 'out_bias_gate': jnp.zeros((N, 1), dtype=jnp.float32), 'loop_gate': jax.random.normal(ks[5], (D, 1), dtype=jnp.float32) * (6.0 / (D + 1)) ** 0.5}
    _L0_gnn_all = _L0_gnn_setup()
    _L0_gnn_in = {k: v for k, v in _L0_gnn_all.items() if k in ('edge_bias', 'gate_weight', 'bias_gate', 'out_edge_bias', 'out_gate_weight', 'out_bias_gate', 'loop_gate')}
    del _L0_gnn_all

    def _L0_ffn_setup():
        import jax, jax.numpy as jnp
        import numpy as np
        TOP_K = 2
        key = jax.random.key(seed)
        ks = jax.random.split(key, 4)
        B, L, D, H, E = (8, 2048, 128, 512, 8)
        s = 0.02
        return {'x': jax.random.normal(ks[0], (B, L, D), jnp.float32), 'Wg': jax.random.normal(ks[1], (D, E), jnp.float32) * s, 'bg': jnp.zeros((E,), jnp.float32), 'W1': jax.random.normal(ks[2], (E, D, H), jnp.float32) * s, 'b1': jnp.zeros((E, H), jnp.float32), 'W2': jax.random.normal(ks[3], (E, H, D), jnp.float32) * s, 'b2': jnp.zeros((E, D), jnp.float32)}
    _L0_ffn_all = _L0_ffn_setup()
    _L0_ffn_in = {k: v for k, v in _L0_ffn_all.items() if k in ('Wg', 'bg', 'W1', 'b1', 'W2', 'b2')}
    del _L0_ffn_all
    return {'x': x, 'adj': adj, 'L0_gnn_edge_bias': _L0_gnn_in['edge_bias'], 'L0_gnn_gate_weight': _L0_gnn_in['gate_weight'], 'L0_gnn_bias_gate': _L0_gnn_in['bias_gate'], 'L0_gnn_out_edge_bias': _L0_gnn_in['out_edge_bias'], 'L0_gnn_out_gate_weight': _L0_gnn_in['out_gate_weight'], 'L0_gnn_out_bias_gate': _L0_gnn_in['out_bias_gate'], 'L0_gnn_loop_gate': _L0_gnn_in['loop_gate'], 'L0_ffn_Wg': _L0_ffn_in['Wg'], 'L0_ffn_bg': _L0_ffn_in['bg'], 'L0_ffn_W1': _L0_ffn_in['W1'], 'L0_ffn_b1': _L0_ffn_in['b1'], 'L0_ffn_W2': _L0_ffn_in['W2'], 'L0_ffn_b2': _L0_ffn_in['b2']}

def reference(x, adj, L0_gnn_edge_bias, L0_gnn_gate_weight, L0_gnn_bias_gate, L0_gnn_out_edge_bias, L0_gnn_out_gate_weight, L0_gnn_out_bias_gate, L0_gnn_loop_gate, L0_ffn_Wg, L0_ffn_bg, L0_ffn_W1, L0_ffn_b1, L0_ffn_W2, L0_ffn_b2):
    import jax
    import jax.numpy as jnp

    def _L0_gnn_ref(label, adj_in, adj_out, edge_bias, gate_weight, bias_gate, out_edge_bias, out_gate_weight, out_bias_gate, loop_gate):
        import jax, jax.numpy as jnp
        import numpy as np
        B, N, D = (2048, 128, 128)
        h = label
        origin = jax.lax.stop_gradient(jnp.where(adj_in <= 0, adj_in, 1.0))
        h_in = jnp.einsum('mn,bnd->bmd', origin * adj_in, h)
        in_gate = jnp.einsum('bnd,do->bno', h, gate_weight) + bias_gate
        msg_in = (h_in + edge_bias) * jax.nn.sigmoid(in_gate)
        h_out = jnp.einsum('mn,bnd->bmd', origin.T * adj_out, h)
        out_gate = jnp.einsum('bnd,do->bno', h, out_gate_weight) + out_bias_gate
        msg_out = (h_out + out_edge_bias) * jax.nn.sigmoid(out_gate)
        lp_gate = jnp.einsum('bnd,do->bno', h, loop_gate)
        msg_loop = h * jax.nn.sigmoid(lp_gate)
        return jax.nn.relu(msg_in + msg_out + msg_loop)

    def _L0_ffn_ref(x, Wg, bg, W1, b1, W2, b2):
        import jax, jax.numpy as jnp
        import numpy as np
        TOP_K = 2
        B, L, D = x.shape
        E = W1.shape[0]
        xf = x.reshape(-1, D)
        gate_logits = xf @ Wg + bg
        top_w, top_i = jax.lax.top_k(gate_logits, TOP_K)
        top_w = jax.nn.softmax(top_w, axis=-1)
        w_dense = jnp.sum(jax.nn.one_hot(top_i, E, dtype=xf.dtype) * top_w[..., None], axis=1)
        out = jnp.zeros_like(xf)
        for e in range(E):
            h = jax.nn.gelu(xf @ W1[e] + b1[e], approximate=False)
            out = out + w_dense[:, e:e + 1] * (h @ W2[e] + b2[e])
        return out.reshape(B, L, D)
    x = x + _L0_gnn_ref(_layernorm(x, axis=-1), adj, adj, L0_gnn_edge_bias, L0_gnn_gate_weight, L0_gnn_bias_gate, L0_gnn_out_edge_bias, L0_gnn_out_gate_weight, L0_gnn_out_bias_gate, L0_gnn_loop_gate)
    x = x + _L0_ffn_ref(_layernorm(x, axis=-1), L0_ffn_Wg, L0_ffn_bg, L0_ffn_W1, L0_ffn_b1, L0_ffn_W2, L0_ffn_b2)
    return x

_drawn_inputs = setup_inputs


def setup_inputs(seed=0):
    import zlib

    import numpy as np

    out = dict(_drawn_inputs(seed))
    spreads = {'L0_gnn_edge_bias': (0.0, 0.555),
     'L0_gnn_bias_gate': (0.0, 0.628),
     'L0_gnn_out_edge_bias': (0.0, 0.557),
     'L0_gnn_out_bias_gate': (0.0, 0.628),
     'L0_ffn_bg': (0.0, 0.554),
     'L0_ffn_b1': (0.0, 0.8),
     'L0_ffn_b2': (0.0, 0.351)}
    factors = {'L0_ffn_W1': 4.59, 'L0_ffn_W2': 4.187}
    for name, (base, spread) in spreads.items():
        noise = np.random.default_rng([zlib.crc32(name.encode()), seed]).standard_normal(out[name].shape)
        drawn = base * np.exp(spread * noise) if base else spread * noise
        out[name] = jnp.asarray(drawn.astype(out[name].dtype))
    for name, factor in factors.items():
        out[name] = (out[name] * factor).astype(out[name].dtype)
    return out
```

```python
from contextlib import ExitStack

import concourse.bass as bass
from concourse import mybir

F32 = mybir.dt.float32
F32R = mybir.dt.float32r
BF16 = mybir.dt.bfloat16
I32 = mybir.dt.int32
U32 = mybir.dt.uint32
ALU = mybir.AluOpType
ACT = mybir.ActivationFunctionType
AX_X = mybir.AxisListType.X

P = 128
G = 8
E = 8
EPS = 1e-5
RSQRT_SEED = float(0x5F3759DF)
FIRST = [(a, b) for a in range(E) for b in range(a + 1, E)]
NCLASS = len(FIRST)
TILE = 256
BLK = TILE // P
ROW = 2 * P + 4


class Turn:

    def __init__(self, group, step, unroll, total):
        self.group, self.step, self.unroll, self.total = group, step, unroll, total
        self.index = group * unroll + step

    def back(self, n):
        return Turn(self.group, self.step - n, self.unroll, self.total)

    def slot(self, ring):
        assert self.unroll % ring == 0
        return self.step % ring

    @property
    def real(self):
        return not isinstance(self.index, int) or 0 <= self.index < self.total


def wait_turn(eng, sem, each, turn, more):
    value = turn.group * (each * turn.unroll) + (each * turn.step + more)
    if not isinstance(value, int) or value > 0:
        eng.wait_ge(sem, value)


def wait_slot(eng, sems, each, turn, more):
    ring = len(sems)
    s = turn.slot(ring)
    wait_turn(eng, sems[s], each, Turn(turn.group, (turn.step - s) // ring, turn.unroll // ring, 0), more)


def apart(eng, sem):
    eng.wait_ge(sem, 1)


def every_turn(eng, unroll, total, body, until=None):
    until = total if until is None else until
    for k in range(unroll):
        body(Turn(0, k, unroll, total))
    with eng.Fori(1, until // unroll) as g:
        for k in range(unroll):
            body(Turn(g, k, unroll, total))
    for k in range(until % unroll):
        body(Turn(until // unroll, k, unroll, total))


class Own:

    def __init__(self, eng, sem):
        self.eng, self.sem, self.base, self.n = eng, sem, 0, 0

    def __call__(self, ins):
        ins.then_inc(self.sem, 1)
        self.n += 1

    def sync(self):
        self.eng.wait_ge(self.sem, self.base + self.n)

    def enter(self, group, first, each):
        self.start, self.each = self.n, each
        self.base = (group * each) + (self.n - first * each)
        self.n = 0

    def leave(self, rounds):
        assert self.n == self.each, (self.n, self.each)
        self.base, self.n = 0, self.start + rounds * self.each


def program(nc, x, adj, edge_bias, gate_weight, bias_gate, out_edge_bias, out_gate_weight,
            out_bias_gate, loop_gate, Wg, bg, W1, b1, W2, b2, out):
    NB, N, D = x.shape
    H = W1.shape[2]
    assert N == P and D == P and NB % (4 * G) == 0 and W1.shape[0] == E
    FC = H // P
    CHUNKS = NB // G
    TOKENS = NB * N
    NT = TOKENS // TILE + NCLASS - 1
    NTG = NT + 1
    COLS = NTG * BLK
    UA, UT = 4, 4
    END = Turn(NT // UT, NT % UT, UT, NT)
    assert CHUNKS % UA == 0

    w_dram = [nc.dram_tensor(f"w{l}_split", (E + 1, P, 2 * H), F32).ap() for l in (1, 2)]
    rows = nc.dram_tensor("rows", (TOKENS + 1, ROW), F32).ap()
    rows_by_node = rows[1:TOKENS + 1, :].rearrange("(n b) k -> n b k", n=N)
    experts_dram = nc.dram_tensor("tile_experts", (NTG, 2), I32).ap()
    x_by_node = x.rearrange("b n d -> n b d")
    out_rows = out.rearrange("b n d -> (b n) d")

    with ExitStack() as ctx:
        def sb(name, shape, dt=F32):
            return ctx.enter_context(nc.sbuf_tensor(name, list(shape), dt))

        def sem(name):
            return ctx.enter_context(nc.semaphore(name))

        bank = ctx.enter_context(nc.psum_tensor("bank", [P, 8, 512], F32))

        ident = sb("ident", [P, P])
        ident_r = sb("ident_r", [P, P], F32R)
        ones_f = sb("ones_f", [P, P])
        before = sb("before", [P, P], BF16)
        ones_b = sb("ones_b", [P, P], BF16)
        zeros_b = sb("zeros_b", [P, COLS], BF16)
        iota_i = sb("iota_i", [P, 256], I32)
        iota_f = sb("iota_f", [P, 256])
        iota_b = sb("iota_b", [P, 256], BF16)
        graph_b = sb("graph_b", [P, NB], BF16)
        node_i = sb("node_i", [P, 1], I32)
        node_f = sb("node_f", [P, 1])
        step_e = sb("step_e", [P, 2, NCLASS])
        keep = sb("keep", [P, NCLASS, G + 1])
        adj_s = sb("adj_s", [P, P])
        adj_t = sb("adj_t", [P, P])
        tmp_m = sb("tmp_m", [P, 2, P])
        adj_in = sb("adj_in", [P, P])
        adj_out = sb("adj_out", [P, P])
        eb = sb("eb", [P, 2, P])
        eb_hi = sb("eb_hi", [P, 2, 4, P], F32R)
        eb_lo = sb("eb_lo", [P, 2, 4, P], F32R)
        gate_w = sb("gate_w", [P, 3])
        gate_b = sb("gate_b", [P, 2])
        wg_s = sb("wg_s", [P, E])
        bg_s = sb("bg_s", [P, E])
        xs = sb("xs", [P, 4, G, D])
        hs = sb("hs", [P, 2, G, D])
        row = sb("row", [P, 2, G, ROW])
        hT = sb("hT", [P, G, P])
        h2T = sb("h2T", [P, G, P])
        t_in = sb("t_in", [P, G, D])
        t_loop = sb("t_loop", [P, G, D])
        t_two = sb("t_two", [P, G, D])
        t_all = sb("t_all", [P, G, D])
        sig = sb("sig", [P, 3, G])
        stats = sb("stats", [P, 2, G, 6])
        ln_tmp = sb("ln_tmp", [P, 2, 8, G])
        ln_bits = sb("ln_bits", [P, 2, 2, G], I32)
        rstd = sb("rstd", [P, 2, G])
        shift = sb("shift", [P, 2, G])
        logit = sb("logit", [P, G, E])
        top = sb("top", [P, G, 8])
        top_at = sb("top_at", [P, G, 8], U32)
        rt = sb("rt", [P, 8, G])
        margin = sb("margin", [P, G])
        hot = sb("hot", [P, NCLASS, G + 1])
        count = sb("count", [P, NCLASS, G + 1])
        ranked = sb("ranked", [P, NCLASS, G])
        class_of = sb("class_of", [P, NB])
        rank_of = sb("rank_of", [P, NB])
        totals = sb("totals", [P, NCLASS], BF16)
        pl = sb("pl", [P, 6, NCLASS])
        pl_i = sb("pl_i", [P, 2, NCLASS], I32)
        pick = sb("pick", [P, 2, G, NCLASS])
        place = sb("place", [P, 2, G])
        place_i = sb("place_i", [P, 3, 2, G], I32)
        at_row = sb("at_row", [P, 2, G, P], BF16)
        at_row_n = sb("at_row_n", [P, 2, G, P], BF16)
        at_row_b = sb("at_row_b", [P, 2, G, P], BF16)
        at_col = sb("at_col", [P, 2, G, COLS], BF16)
        inv = sb("inv", [P, 4, COLS])
        index = sb("index", [P, NTG, 2 * BLK], I32)
        started = sb("started", [P, 2, NCLASS])
        steps = sb("steps", [P, 4, NCLASS])
        node_b = sb("node_b", [P, 2])
        expert = sb("expert", [P, 4])
        change = sb("change", [P, 3, 2])
        code = sb("code", [P, 2], I32)
        expert_rep = sb("expert_rep", [P, 2, E])
        expert_hot = sb("expert_hot", [E, 2, P])
        b_of_tile = sb("b_of_tile", [P, FC + 1, 2, P])
        zero_row = sb("zero_row", [1, ROW])
        w_in = sb("w_in", [P, 2, 2, H])
        w_split = sb("w_split", [P, 2, 2, 2, H], F32R)
        b1_s = sb("b1_s", [E, H])
        b2_s = sb("b2_s", [E, D])
        wt = [sb(f"wt{l}", [P, 2, 2 * H], F32R) for l in (1, 2)]
        b_t = sb("b_t", [P, UT, FC + 1, 2])
        from_row = sb("from_row", [P, UT, BLK], I32)
        to_row = sb("to_row", [P, UT, BLK], I32)
        got = sb("got", [P, UT, BLK, ROW])
        in_hi = sb("in_hi", [P, 2, TILE], F32R)
        in_lo = sb("in_lo", [P, 2, TILE], F32R)
        act_f = sb("act_f", [P, 2, FC, TILE])
        act_hi = sb("act_hi", [P, 2, FC, TILE], F32R)
        act_lo = sb("act_lo", [P, 2, FC, TILE], F32R)
        y_t = sb("y_t", [P, 2, TILE])
        y_one = sb("y_one", [P, BLK, D])
        y_out = sb("y_out", [P, UT, BLK, D])

        ps_t = bank[:, 0:2, :].rearrange("p k (g m) -> p k g m", g=4)
        ps_in = bank[:, 2:4, :].rearrange("p k (g m) -> p k g m", g=4)
        ps_out = bank[:, 4:6, :].rearrange("p k (g m) -> p k g m", g=4)
        ps_gate = bank[:, 6, 0:4 * G].rearrange("p (g k) -> p g k", k=4)
        ps_logit = bank[:, 6, 64:64 + G * E].rearrange("p (g e) -> p g e", e=E)
        ps_pre = bank[:, 7, 0:NCLASS]
        ps_tot = bank[:, 7, 64:64 + NCLASS]
        ps_a = bank[:, 0, 0:COLS]
        ps_b = bank[:, 1, 0:COLS]
        ps_h = [bank[:, 2 * s:2 * s + 2, :].rearrange("p k (c m) -> p (k c) m", m=TILE) for s in range(2)]
        ps_y = [bank[:, 4 + s, 0:TILE] for s in range(2)]
        ps_x = bank[:, 6, 0:TILE]
        ps_o = bank[:, 7, :].rearrange("p (s j m) -> p s j m", s=2, j=BLK)
        ps_exp = bank[0:E, 2, 0:2 * P].rearrange("p (s t) -> p s t", s=2)
        ps_bias = bank[:, 4:7, :].rearrange("p k (c s t) -> p (k c) s t", s=2, t=P)[:, 0:FC + 1]

        s_const = sem("pool_constants")
        s_iota = sem("iota_copies")
        s_small = sem("small_inputs_loaded")
        s_bias = sem("biases_loaded")
        s_adjt = sem("adj_transposed")
        s_adj = sem("adj_matrices_ready")
        s_x = [sem(f"x_loaded{i}") for i in range(4)]
        s_ln1 = sem("ln1_ready")
        s_h = sem("h_ready")
        s_ht_ps = sem("hT_in_psum")
        s_ht = sem("hT_copied")
        s_gate = sem("gates_in_psum")
        s_prod = sem("products_in_psum")
        s_sig = sem("sigmoids_ready")
        s_tin = sem("t_in_ready")
        s_two = sem("t_two_ready")
        s_comb = sem("sum_ready")
        s_x1 = sem("x1_ready")
        s_ln2 = sem("ln2_ready")
        s_h2 = sem("h2_ready")
        s_h2t_ps = sem("h2T_in_psum")
        s_h2t = sem("h2T_copied")
        s_logit = sem("logits_in_psum")
        s_lsum = sem("logits_read")
        s_margin = sem("margins_ready")
        s_rw = sem("row_weights_ready")
        s_row = [sem(f"row_stored{i}") for i in range(2)]
        s_dve = sem("dve_own")
        s_pool = sem("pool_own")
        s_tot = sem("totals_ready")
        s_tot_ps = sem("totals_in_psum")
        s_hot = sem("one_hots_ready")
        s_hot_c = sem("column_hots_ready")
        s_hot_n = sem("row_hots_times_node")
        s_hot_b = sem("row_hots_times_graph")
        s_inv = sem("inverse_products")
        s_index = sem("index_ready")
        s_texp = sem("tile_experts_ready")
        s_tab = sem("tile_experts_stored")
        s_wl = [sem(f"w_staged{i}") for i in range(2)]
        s_whi = sem("w_hi_ready")
        s_wlo = sem("w_lo_ready")
        s_ws = [sem(f"w_split_stored{i}") for i in range(2)]
        s_bs = sem("zero_row_stored")
        s_rep = sem("tile_experts_repeated")
        s_exp_ps = sem("tile_experts_on_all_partitions")
        s_exp_hot = sem("tile_experts_one_hot")
        s_b_ps = sem("b_of_tiles_in_psum")
        s_btab = sem("b_of_tiles_copied")
        s_wt = [[sem(f"w{l}_of_slot{s}") for s in range(2)] for l in (1, 2)]
        s_first = sem("first_gather_indices_copied")
        s_from = [sem(f"gather_index_copied{i}") for i in range(UT)]
        s_to = [sem(f"scatter_index_copied{i}") for i in range(UT)]
        s_got = [sem(f"rows_gathered{i}") for i in range(UT)]
        s_xt = sem("tile_transposed")
        s_inhi = sem("tile_hi")
        s_inlo = sem("tile_lo")
        s_mm1 = [sem(f"hidden_in_psum{s}") for s in range(2)]
        s_act = [sem(f"gelu_done{s}") for s in range(2)]
        s_hhi = sem("hidden_hi")
        s_split = [sem(f"hidden_split{s}") for s in range(2)]
        s_mm2 = [sem(f"expert_out_in_psum{s}") for s in range(2)]
        s_y = [sem(f"expert_out_copied{s}") for s in range(2)]
        s_o = sem("outputs_transposed")
        s_bt = [sem(f"tile_b1_copied{i}") for i in range(UT)]
        s_y1 = sem("first_expert_added")
        s_done = [sem(f"tile_summed{i}") for i in range(UT)]
        s_out = [sem(f"rows_scattered{i}") for i in range(UT)]
        N_CONST = 14

        block = ctx.enter_context(nc.Block())

        @block.sync
        def _(sp):
            sp.dma_start(adj_s[:], adj).then_inc(s_small, 16)
            sp.dma_start(eb[:, 0, :], edge_bias).then_inc(s_small, 16)
            sp.dma_start(eb[:, 1, :], out_edge_bias).then_inc(s_small, 16)

            def load_x(t):
                if t.real:
                    wait_turn(sp, s_x1, 1, t.back(4), 1)
                    b = t.index * G
                    sp.dma_start(xs[:, t.slot(4)], x_by_node[:, bass.ds(b, G), :]).then_inc(s_x[t.slot(4)], 16)

            for k in range(UA):
                load_x(Turn(0, k, UA, CHUNKS))
            for k, w in enumerate((gate_weight, out_gate_weight, loop_gate)):
                sp.dma_start(gate_w[:, k:k + 1], w).then_inc(s_small, 16)
            sp.dma_start(gate_b[:, 0:1], bias_gate).then_inc(s_small, 16)
            sp.dma_start(gate_b[:, 1:2], out_bias_gate).then_inc(s_small, 16)
            sp.dma_start(wg_s[:], Wg).then_inc(s_small, 16)
            sp.dma_start(bg_s[:], bg.partition_broadcast(P)).then_inc(s_small, 16)
            sp.dma_start(b1_s[:], b1).then_inc(s_bias, 16)
            sp.dma_start(b2_s[:], b2).then_inc(s_bias, 16)

            def w_source(k):
                layer, e = k // (E // 2), 2 * (k % (E // 2))
                if layer == 0:
                    return W1[e:e + 2].rearrange("e p h -> p e h")
                return W2[e:e + 2].rearrange("e (c p) d -> p e c d", p=P)

            def load_w(k):
                if k >= 2:
                    sp.wait_ge(s_wlo, k - 1)
                dst = w_in[:, k % 2]
                if k >= E // 2:
                    dst = dst.rearrange("p e (c d) -> p e c d", c=FC)
                src = w_source(k)
                for e in range(2):
                    sp.dma_start(dst[:, e], src[:, e]).then_inc(s_wl[k % 2], 16)

            def store_w(k):
                layer, e = k // (E // 2), 2 * (k % (E // 2))
                sp.wait_ge(s_wlo, k + 1)
                dst = w_dram[layer][e:e + 2].rearrange("e p h -> p e h")
                sp.dma_start(dst, w_split[:, k % 2].bitcast(F32).rearrange("p e k h -> p e (k h)")).then_inc(s_ws[k % 2], 16)

            load_w(0)
            load_w(1)

            for w in range(E):
                store_w(w)
                if w + 2 < E:
                    load_w(w + 2)
            sp.wait_ge(s_const, N_CONST)
            sp.dma_start(rows[0:1, :], zero_row[:]).then_inc(s_bs, 16)
            with sp.Fori(1, CHUNKS // UA) as g:
                for k in range(UA):
                    load_x(Turn(g, k, UA, CHUNKS))

            sp.wait_ge(s_texp, 1)
            sp.dma_start(experts_dram, code[0:NTG, :]).then_inc(s_tab, 16)
            sp.wait_ge(s_tab, 16)
            for i in range(2):
                sp.wait_ge(s_ws[i], 16 * E // 2)
            sp.wait_ge(s_bs, 16)

            def weights(t):
                new = [sp.value_load(experts_dram[bass.ds(t.index, 1), s:s + 1], min_val=0, max_val=E) for s in range(2)]
                for s in range(2):
                    with sp.If_ne(new[s].val, E):
                        wait_turn(sp, s_mm1[s], 2, t, 0)
                        sp.dma_start(wt[0][:, s, :].bitcast(F32), w_dram[0][bass.ds(new[s], 1)].rearrange("a p h -> (a p) h")).then_inc(s_wt[0][s], 16)
                    with sp.Else():
                        wait_turn(sp, s_mm1[s], 2, t, 0)
                        sp.sem_inc(s_wt[0][s], 16)
                for s in range(2):
                    with sp.If_ne(new[s].val, E):
                        wait_turn(sp, s_mm2[s], 1, t, 0)
                        sp.dma_start(wt[1][:, s, :].bitcast(F32), w_dram[1][bass.ds(new[s], 1)].rearrange("a p h -> (a p) h")).then_inc(s_wt[1][s], 16)
                    with sp.Else():
                        wait_turn(sp, s_mm2[s], 1, t, 0)
                        sp.sem_inc(s_wt[1][s], 16)

            every_turn(sp, UT, NT, weights)
            for i in range(UT):
                sp.wait_ge(s_out[i], 16 * BLK * ((NT + UT - 1 - i) // UT))

        @block.gpsimd
        def _(pool):
            own = Own(pool, s_pool)
            pool.memset(ones_f[:], 1.0).then_inc(s_const, 1)
            pool.memset(ident[:], 0.0).then_inc(s_const, 1)
            pool.memset(ones_b[:], 1.0).then_inc(s_const, 1)
            pool.memset(zeros_b[:], 0.0).then_inc(s_const, 1)
            pool.memset(keep[:], 1.0).then_inc(s_const, 1)
            pool.memset(step_e[:, 0, :], 0.0).then_inc(s_const, 1)
            pool.memset(step_e[:, 1, :], 1.0).then_inc(s_const, 1)
            pool.memset(zero_row[:], 0.0).then_inc(s_const, 1)
            pool.iota(iota_i[:], pattern=[[1, 256]], base=0, channel_multiplier=0).then_inc(s_const, 1)
            pool.iota(node_i[:], pattern=[[0, 1]], base=0, channel_multiplier=1).then_inc(s_const, 1)
            pool.wait_ge(s_const, 10)
            pool.affine_select(out=ident[:], in_=ident[:], pattern=[[-1, P]], compare_op=ALU.not_equal,
                               fill=1.0, base=0, channel_multiplier=1).then_inc(s_const, 1)
            pool.affine_select(out=before[:], in_=ones_b[:], pattern=[[1, P]], compare_op=ALU.is_gt,
                               fill=0.0, base=0, channel_multiplier=-1).then_inc(s_const, 1)
            pool.memset(keep[:, :, 0:1], 0.0).then_inc(s_const, 1)
            for c in range(1, NCLASS):
                for s in range(2):
                    d = FIRST[c][s] - FIRST[c - 1][s]
                    if d != s:
                        own(pool.memset(step_e[:, s, c:c + 1], float(d)))
            own.sync()
            pool.memset(row[:, :, :, 2 * P:ROW], 0.0).then_inc(s_const, 1)

            def mix(t):
                if t.real:
                    wait_turn(pool, s_sig, 1, t, 1)
                    wait_turn(pool, s_two, 1, t, 0)
                    gate = sig[:, 2, :].unsqueeze(2).to_broadcast([P, G, D])
                    own(pool.tensor_tensor(t_loop[:], hs[:, t.slot(2)], gate, ALU.mult))
                    own.sync()
                    wait_turn(pool, s_tin, 1, t, 1)
                    wait_turn(pool, s_comb, 1, t, 0)
                    pool.tensor_tensor(t_two[:], t_loop[:], t_in[:], ALU.add).then_inc(s_two, 1)

            def split_lo(k):
                pool.wait_ge(s_whi, k + 1)
                for e in range(2):
                    last = pool.tensor_tensor(w_split[:, k % 2, e, 1], w_in[:, k % 2, e],
                                              w_split[:, k % 2, e, 0].bitcast(F32), ALU.subtract)
                last.then_inc(s_wlo, 1)

            for k in range(UA):
                for w in (2 * k, 2 * k + 1):
                    if w >= 2:
                        pool.wait_ge(s_ws[w % 2], 16 * (w // 2))
                    split_lo(w)
                mix(Turn(0, k, UA, CHUNKS).back(1))
            with pool.Fori(1, CHUNKS // UA) as g:
                own.enter(g, 1, UA)
                for k in range(UA):
                    mix(Turn(g, k, UA, CHUNKS).back(1))
                own.leave(CHUNKS // UA - 1)
            mix(Turn(CHUNKS // UA, 0, UA, CHUNKS).back(1))

            def times_graph(t, b):
                wait_turn(pool, s_hot, 1, t, 1)
                wait_turn(pool, s_inv, 1, t, -1)
                pool.tensor_tensor(at_row_b[:, t.slot(2)], at_row[:, t.slot(2)],
                                   graph_b[:, bass.ds(b, G)].unsqueeze(2).to_broadcast([P, G, P]),
                                   ALU.mult).then_inc(s_hot_b, 1)

            pool.wait_ge(s_iota, 6)
            for k in range(2):
                times_graph(Turn(0, k, 2, CHUNKS), k * G)
            with pool.Fori(1, CHUNKS // 2) as g:
                for k in range(2):
                    t = Turn(g, k, 2, CHUNKS)
                    times_graph(t, t.index * G)

            pool.wait_ge(s_index, 1)
            pool.wait_ge(s_btab, 1)
            pool.wait_ge(s_bs, 16)
            for i in range(2):
                pool.wait_ge(s_row[i], 16 * CHUNKS // 2)

            def gather(t, copied):
                s = t.slot(UT)
                wait_slot(pool, s_done, 1, t.back(UT), 1)
                wait_slot(pool, s_got, 16 * BLK, t, 0)
                pool.tensor_copy(from_row[:, s, :], index[:, bass.ds(t.index, 1), 0:BLK].rearrange("p a k -> p (a k)")).then_inc(copied, 1)
                pool.tensor_copy(b_t[:, s], b_of_tile[:, :, :, bass.ds(t.index, 1)].rearrange("p c s a -> p c (s a)")).then_inc(s_bt[s], 1)
                apart(pool, s_const)
                if copied is s_first:
                    pool.wait_ge(s_first, t.index + 1)
                else:
                    wait_slot(pool, s_from, 1, t.back(UT), 1)
                for j in range(BLK):
                    pool.indirect_dma_start(out=got[:, s, j, :], out_offset=None, in_=rows,
                                            in_offset=bass.IndirectOffsetOnAxis(ap=from_row[:, s, j:j + 1], axis=0)).then_inc(s_got[s], 16)

            def scatter(t):
                s = t.slot(UT)
                wait_slot(pool, s_done, 1, t, 1)
                wait_slot(pool, s_out, 16 * BLK, t, 0)
                pool.tensor_copy(to_row[:, s, :], index[:, bass.ds(t.index, 1), BLK:2 * BLK].rearrange("p a k -> p (a k)")).then_inc(s_to[s], 1)
                apart(pool, s_const)
                wait_slot(pool, s_to, 1, t, 1)
                for j in range(BLK):
                    pool.indirect_dma_start(out=out_rows, out_offset=bass.IndirectOffsetOnAxis(ap=to_row[:, s, j:j + 1], axis=0),
                                            in_=y_out[:, s, j, :], in_offset=None, bounds_check=TOKENS - 1,
                                            oob_is_err=False).then_inc(s_out[s], 16)

            def move(t):
                scatter(t)
                gather(Turn(t.group, t.step + UT, UT, NT), s_from[t.slot(UT)])

            for k in range(UT):
                gather(Turn(0, k, UT, NT), s_first)
            every_turn(pool, UT, NT, move, NTG - UT)
            for t in range(NTG - UT, NT):
                scatter(Turn(t // UT, t % UT, UT, NT))

        @block.scalar
        def _(act):
            def split_hi(k):
                act.wait_ge(s_wl[k % 2], 32 * (k // 2 + 1))
                if k >= 2:
                    act.wait_ge(s_ws[k % 2], 16 * (k // 2))
                for e in range(2):
                    last = act.activation(w_split[:, k % 2, e, 0], w_in[:, k % 2, e], ACT.Copy)
                last.then_inc(s_whi, 1)

            def gates(t):
                if t.real:
                    wait_turn(act, s_gate, 1, t, 1)
                    wait_turn(act, s_comb, 1, t, 0)
                    wait_turn(act, s_two, 1, t, 0)
                    for k in range(3):
                        bias = gate_b[:, k:k + 1] if k < 2 else 0.0
                        last = act.activation(sig[:, k, :], ps_gate[:, :, k], ACT.Sigmoid, bias=bias)
                    last.then_inc(s_sig, 1)

            def times_in(t):
                if t.real:
                    wait_turn(act, s_prod, 1, t, 1)
                    wait_turn(act, s_sig, 1, t, 1)
                    for b in range(G):
                        last = act.activation(t_in[:, b, :], ps_in[:, b // 4, b % 4, :], ACT.Copy, scale=sig[:, 0, b:b + 1])
                    last.then_inc(s_tin, 1)

            def norm1(t):
                if t.real:
                    wait_turn(act, s_ln1, 1, t, 1)
                    wait_turn(act, s_prod, 1, t, -1)
                    wait_turn(act, s_two, 1, t, -1)
                    for b in range(G):
                        last = act.activation(hs[:, t.slot(2), b, :], xs[:, t.slot(4), b, :], ACT.Identity,
                                              scale=rstd[:, 0, b:b + 1], bias=shift[:, 0, b:b + 1])
                    last.then_inc(s_h, 1)

            def norm2(t):
                if t.real:
                    wait_turn(act, s_ln2, 1, t, 1)
                    for b in range(G):
                        last = act.activation(row[:, t.slot(2), b, 0:P], row[:, t.slot(2), b, P:2 * P], ACT.Identity,
                                              scale=rstd[:, 1, b:b + 1], bias=shift[:, 1, b:b + 1])
                    last.then_inc(s_h2, 1)

            def copy_t(t, s_from, s_done_, dst, s_free):
                if t.real:
                    wait_turn(act, s_free, 1, t, 0)
                    for k in range(2):
                        wait_turn(act, s_from, 2, t, k + 1)
                        act.activation(dst[:, 4 * k:4 * k + 4, :], ps_t[:, k], ACT.Copy).then_inc(s_done_, 1)

            def row_weights(t):
                if t.real:
                    wait_turn(act, s_margin, 1, t, 1)
                    act.activation(row[:, t.slot(2), :, 2 * P], margin[:], ACT.Sigmoid)
                    act.activation(row[:, t.slot(2), :, 2 * P + 1], margin[:], ACT.Sigmoid, scale=-1.0).then_inc(s_rw, 1)

            def store_row(t):
                if t.real:
                    wait_turn(act, s_rw, 1, t, 1)
                    b = t.index * G
                    act.dma_start(rows_by_node[:, bass.ds(b, G), :], row[:, t.slot(2)]).then_inc(s_row[t.slot(2)], 16)

            def chunk(t):
                gates(t.back(1))
                times_in(t.back(1))
                norm1(t)
                copy_t(t.back(2), s_h2t_ps, s_h2t, h2T, s_logit)
                copy_t(t, s_ht_ps, s_ht, hT, s_gate)
                row_weights(t.back(2))
                store_row(t.back(2))
                norm2(t.back(1))

            act.wait_ge(s_small, 16 * 10)
            act.wait_ge(s_const, N_CONST)
            act.activation(ident_r[:], ident[:], ACT.Copy).then_inc(s_adj, 1)
            for k in range(UA):
                split_hi(2 * k)
                split_hi(2 * k + 1)
                chunk(Turn(0, k, UA, CHUNKS))
            with act.Fori(1, CHUNKS // UA) as g:
                for k in range(UA):
                    chunk(Turn(g, k, UA, CHUNKS))
            for k in range(2):
                chunk(Turn(CHUNKS // UA, k, UA, CHUNKS))

            def times_node(t):
                wait_turn(act, s_hot, 1, t, 1)
                wait_turn(act, s_inv, 1, t, -1)
                act.activation(at_row_n[:, t.slot(2)], at_row[:, t.slot(2)], ACT.Copy, scale=node_f[:]).then_inc(s_hot_n, 1)

            act.wait_ge(s_iota, 6)
            for k in range(2):
                times_node(Turn(0, k, 2, CHUNKS))
            with act.Fori(1, CHUNKS // 2) as g:
                for k in range(2):
                    times_node(Turn(g, k, 2, CHUNKS))

            act.wait_ge(s_b_ps, 1)
            act.activation(b_of_tile[:], ps_bias, ACT.Copy).then_inc(s_btab, 1)

            def tile_hi(t):
                wait_turn(act, s_xt, 1, t, 1)
                wait_turn(act, s_mm1[1], 2, t, -2)
                act.activation(in_hi[:, t.slot(2)], ps_x, ACT.Copy).then_inc(s_inhi, 1)

            def gelu(t, s):
                wait_turn(act, s_split[s], 2, t, 0)
                if s == 0:
                    wait_slot(act, s_bt, 1, t, 1)
                for c in range(FC):
                    if c % 2 == 0:
                        wait_turn(act, s_mm1[s], 2, t, c // 2 + 1)
                    act.activation(act_f[:, s, c, :], ps_h[s][:, c, :], ACT.Gelu, bias=b_t[:, t.slot(UT), c, s:s + 1]).then_inc(s_act[s], 1)

            def copy_y(t, s):
                if t.real:
                    wait_turn(act, s_mm2[s], 1, t, 1)
                    wait_turn(act, s_o, 1, t, 0)
                    act.activation(y_t[:, s, :], ps_y[s], ACT.Identity, bias=b_t[:, t.slot(UT), FC, s:s + 1]).then_inc(s_y[s], 1)

            def tile(t):
                gelu(t, 0)
                copy_y(t.back(1), 1)
                tile_hi(Turn(t.group, t.step + 1, UT, NT))
                gelu(t, 1)
                copy_y(t, 0)

            tile_hi(Turn(0, 0, UT, NT))
            every_turn(act, UT, NT, tile)
            copy_y(END.back(1), 1)

        @block.vector
        def _(dve):
            own = Own(dve, s_dve)

            dve.wait_ge(s_const, N_CONST)
            dve.tensor_copy(iota_f[:], iota_i[:]).then_inc(s_iota, 1)
            dve.tensor_copy(iota_b[:], iota_i[:]).then_inc(s_iota, 1)
            dve.tensor_scalar(graph_b[:], iota_i[:, 0:NB], 1.0, None, ALU.add).then_inc(s_iota, 1)
            dve.tensor_copy(node_f[:], node_i[:]).then_inc(s_iota, 1)
            dve.tensor_scalar(node_b[:, 0:1], node_i[:], -1.0, None, ALU.add).then_inc(s_iota, 1)
            dve.tensor_scalar(node_b[:, 1:2], node_i[:], 0.0, None, ALU.is_equal).then_inc(s_iota, 1)

            dve.wait_ge(s_small, 16 * 10)
            dve.wait_ge(s_adjt, 1)
            own(dve.tensor_copy(adj_t[:], ps_t[:, 0, 0, :]))
            own(dve.scalar_tensor_tensor(out=tmp_m[:, 1, :], in0=adj_s[:], scalar=0.0, in1=adj_s[:], op0=ALU.is_le, op1=ALU.mult))
            own.sync()
            own(dve.scalar_tensor_tensor(out=tmp_m[:, 0, :], in0=adj_t[:], scalar=0.0, in1=adj_t[:], op0=ALU.is_le, op1=ALU.mult))
            own.sync()
            own(dve.scalar_tensor_tensor(out=adj_out[:], in0=adj_s[:], scalar=0.0, in1=tmp_m[:, 1, :], op0=ALU.is_gt, op1=ALU.add))
            own(dve.scalar_tensor_tensor(out=adj_in[:], in0=adj_t[:], scalar=0.0, in1=tmp_m[:, 0, :], op0=ALU.is_gt, op1=ALU.add))
            own.sync()
            own(dve.tensor_tensor(tmp_m[:, 0, :], adj_in[:], adj_t[:], ALU.mult))
            own(dve.tensor_tensor(tmp_m[:, 1, :], adj_out[:], adj_t[:], ALU.mult))
            own.sync()
            dve.tensor_copy(adj_in[:], tmp_m[:, 0, :]).then_inc(s_adj, 1)
            dve.tensor_copy(adj_out[:], tmp_m[:, 1, :]).then_inc(s_adj, 1)
            for k in range(2):
                src = eb[:, k, :].unsqueeze(1).to_broadcast([P, 4, P])
                own(dve.tensor_copy(eb_hi[:, k], src))
                own.sync()
                dve.tensor_tensor(eb_lo[:, k], src, eb_hi[:, k].bitcast(F32), ALU.subtract).then_inc(s_adj, 1)

            def layer_norm(which, source, done):
                a = ln_tmp[:, which]
                st = stats[:, which]
                for b in range(G):
                    own(dve.bn_stats(st[:, b, :], source(b)))
                own.sync()
                msum, mdiff, m2, dd, var, y, t1_, t2_ = (a[:, i, :] for i in range(8))
                own(dve.tensor_tensor(msum, st[:, :, 1], st[:, :, 4], ALU.add))
                own(dve.tensor_tensor(mdiff, st[:, :, 1], st[:, :, 4], ALU.subtract))
                own(dve.tensor_tensor(m2, st[:, :, 2], st[:, :, 5], ALU.add))
                own.sync()
                own(dve.tensor_tensor(dd, mdiff, mdiff, ALU.mult))
                own.sync()
                own(dve.scalar_tensor_tensor(out=t1_, in0=dd, scalar=D / 4.0, in1=m2, op0=ALU.mult, op1=ALU.add))
                own.sync()
                own(dve.tensor_scalar(var, t1_, 1.0 / D, EPS, ALU.mult, ALU.add))
                own.sync()
                own(dve.tensor_scalar(ln_bits[:, which, 0, :], var.bitcast(I32), 1, None, ALU.logical_shift_right))
                own.sync()
                own(dve.tensor_scalar(ln_bits[:, which, 1, :], ln_bits[:, which, 0, :], -1.0, RSQRT_SEED, ALU.mult, ALU.add))
                own.sync()
                now = ln_bits[:, which, 1, :].bitcast(F32)
                for i in range(3):
                    own(dve.tensor_tensor(t1_, now, now, ALU.mult))
                    own.sync()
                    own(dve.scalar_tensor_tensor(out=t2_, in0=t1_, scalar=-0.5, in1=var, op0=ALU.mult, op1=ALU.mult))
                    own.sync()
                    nxt = (y, dd, rstd[:, which, :])[i]
                    own(dve.scalar_tensor_tensor(out=nxt, in0=t2_, scalar=1.5, in1=now, op0=ALU.add, op1=ALU.mult))
                    own.sync()
                    now = nxt
                dve.scalar_tensor_tensor(out=shift[:, which, :], in0=msum, scalar=-0.5, in1=now,
                                         op0=ALU.mult, op1=ALU.mult).then_inc(done, 1)

            def first_norm(t):
                if t.real:
                    wait_turn(dve, s_x[t.slot(4)], 16, Turn(t.group, 0, 1, 0), 16)
                    wait_turn(dve, s_h, 1, t, 0)
                    layer_norm(0, lambda b: xs[:, t.slot(4), b, :], s_ln1)

            def add_up(t):
                if t.real:
                    wait_turn(dve, s_two, 1, t, 1)
                    wait_turn(dve, s_prod, 1, t, 1)
                    wait_turn(dve, s_x1, 1, t, 0)
                    for b in range(G):
                        last = dve.scalar_tensor_tensor(out=t_all[:, b, :], in0=ps_out[:, b // 4, b % 4, :],
                                                        scalar=sig[:, 1, b:b + 1], in1=t_two[:, b, :],
                                                        op0=ALU.mult, op1=ALU.add)
                    last.then_inc(s_comb, 1)
                    wait_turn(dve, s_comb, 1, t, 1)
                    wait_turn(dve, s_row[t.slot(2)], 16, Turn(t.group, (t.step - t.slot(2)) // 2, UA // 2, 0), 0)
                    dve.scalar_tensor_tensor(out=row[:, t.slot(2), :, P:2 * P], in0=t_all[:], scalar=0.0,
                                             in1=xs[:, t.slot(4)], op0=ALU.max, op1=ALU.add).then_inc(s_x1, 1)

            def second_norm(t):
                if t.real:
                    wait_turn(dve, s_x1, 1, t, 1)
                    wait_turn(dve, s_h2, 1, t, 0)
                    layer_norm(1, lambda b: row[:, t.slot(2), b, P:2 * P], s_ln2)

            def route(t):
                if not t.real:
                    return
                b0 = t.index * G
                wait_turn(dve, s_logit, 1, t, 1)
                dve.tensor_tensor(logit[:], ps_logit, bg_s[:].unsqueeze(1).to_broadcast([P, G, E]), ALU.add).then_inc(s_lsum, 1)
                apart(dve, s_const)
                wait_turn(dve, s_lsum, 1, t, 1)
                for b in range(G):
                    own(dve.max(top[:, b, :], logit[:, b, :]))
                own.sync()
                own(dve.tensor_tensor(rt[:, 4, :], top[:, :, 0], top[:, :, 1], ALU.subtract))
                for b in range(G):
                    own(dve.max_index(top_at[:, b, :], top[:, b, :], logit[:, b, :]))
                own.sync()
                i0, i1 = top_at[:, :, 0], top_at[:, :, 1]
                low, high, order, sign, diff, half, prod = (rt[:, i, :] for i in range(7))
                own(dve.tensor_tensor(low, i0, i1, ALU.min))
                own(dve.tensor_tensor(high, i0, i1, ALU.max))
                own(dve.tensor_tensor(order, i0, i1, ALU.is_lt))
                own.sync()
                own(dve.tensor_scalar(sign, order, 2.0, -1.0, ALU.mult, ALU.add))
                own(dve.tensor_scalar(half, low, -0.5, E - 1.5, ALU.mult, ALU.add))
                own.sync()
                wait_turn(dve, s_rw, 1, t, 0)
                dve.tensor_tensor(margin[:], diff, sign, ALU.mult).then_inc(s_margin, 1)
                own(dve.tensor_tensor(prod, half, low, ALU.mult))
                own.sync()
                own(dve.scalar_tensor_tensor(out=rt[:, 7, :], in0=prod, scalar=-1.0, in1=high, op0=ALU.add, op1=ALU.add))
                own.sync()
                own(dve.tensor_copy(class_of[:, bass.ds(b0, G)], rt[:, 7, :]))
                own(dve.tensor_copy(hot[:, :, 0:1], count[:, :, G:G + 1]))
                own(dve.tensor_tensor(hot[:, :, 1:G + 1], iota_f[:, 0:NCLASS].unsqueeze(2).to_broadcast([P, NCLASS, G]),
                                      rt[:, 7, :].unsqueeze(1).to_broadcast([P, NCLASS, G]), ALU.is_equal))
                own.sync()
                own(dve.tensor_tensor_scan(count[:].rearrange("p c g -> p (c g)"), keep[:].rearrange("p c g -> p (c g)"),
                                           hot[:].rearrange("p c g -> p (c g)"), 0.0, ALU.mult, ALU.add))
                own.sync()
                own(dve.tensor_tensor(ranked[:], hot[:, :, 1:G + 1], count[:, :, 0:G], ALU.mult))
                own.sync()
                own(dve.tensor_reduce(rank_of[:, bass.ds(b0, G)], ranked[:].rearrange("p c g -> p g c"), AX_X, ALU.add))

            def chunk(t):
                first_norm(t)
                route(t.back(2))
                add_up(t.back(1))
                second_norm(t.back(1))

            own(dve.memset(count[:], 0.0))
            own.sync()
            for k in range(UA):
                n0 = own.n
                chunk(Turn(0, k, UA, CHUNKS))
                each = own.n - n0
            with dve.Fori(1, CHUNKS // UA) as g:
                own.enter(g, 1, UA * each)
                for k in range(UA):
                    chunk(Turn(g, k, UA, CHUNKS))
                own.leave(CHUNKS // UA - 1)
            for k in range(2):
                chunk(Turn(CHUNKS // UA, k, UA, CHUNKS))

            own.sync()
            dve.tensor_copy(totals[:], count[:, :, G]).then_inc(s_tot, 1)
            dve.wait_ge(s_tot_ps, 1)
            tiles_f, upto, base, offset, ones_c = (pl[:, i, :] for i in range(5))
            own(dve.tensor_scalar(pl_i[:, 0, :], ps_tot, TILE - 1.0, None, ALU.add))
            own(dve.memset(ones_c, 1.0))
            own.sync()
            own(dve.tensor_scalar(pl_i[:, 1, :], pl_i[:, 0, :], TILE.bit_length() - 1, None, ALU.logical_shift_right))
            own.sync()
            own(dve.tensor_copy(tiles_f, pl_i[:, 1, :]))
            own.sync()
            own(dve.tensor_tensor_scan(upto, ones_c, tiles_f, 0.0, ALU.mult, ALU.add))
            own.sync()
            own(dve.tensor_tensor(base, upto, tiles_f, ALU.subtract))
            own.sync()
            own(dve.scalar_tensor_tensor(out=offset, in0=base, scalar=float(TILE), in1=ps_pre, op0=ALU.mult, op1=ALU.add))
            own(dve.tensor_scalar(started[:, 0, :], base, node_f[:], None, ALU.is_le))
            own(dve.tensor_scalar(started[:, 1, :], base, node_b[:, 0:1], None, ALU.is_le))
            own.sync()
            for k in range(2):
                for s in range(2):
                    own(dve.tensor_tensor(steps[:, 2 * k + s, :], started[:, k, :], step_e[:, s, :], ALU.mult))
            own.sync()
            own(dve.tensor_reduce(expert[:], steps[:], AX_X, ALU.add))
            own.sync()
            dve.tensor_copy(expert_rep[:], expert[:, 0:2].unsqueeze(2).to_broadcast([P, 2, E])).then_inc(s_rep, 1)
            own(dve.tensor_tensor(change[:, 0, :], expert[:, 0:2], expert[:, 2:4], ALU.subtract))
            own.sync()
            own(dve.tensor_tensor(change[:, 1, :], change[:, 0, :], change[:, 0, :], ALU.mult))
            own.sync()
            own(dve.tensor_scalar(change[:, 2, :], change[:, 1, :], node_b[:, 1:2], 0.0, ALU.add, ALU.is_gt))
            own.sync()
            own(dve.scalar_tensor_tensor(out=change[:, 0, :], in0=expert[:, 0:2], scalar=-float(E), in1=change[:, 2, :], op0=ALU.add, op1=ALU.mult))
            own.sync()
            dve.tensor_scalar(code[:], change[:, 0, :], float(E), None, ALU.add).then_inc(s_texp, 1)
            dve.wait_ge(s_exp_ps, 1)
            dve.tensor_scalar(expert_hot[:], ps_exp, node_f[0:E, :], None, ALU.is_equal).then_inc(s_exp_hot, 1)

            def one_hots(t, b0):
                s = t.slot(2)
                own(dve.tensor_tensor(pick[:, 0], iota_f[:, 0:NCLASS].unsqueeze(1).to_broadcast([P, G, NCLASS]),
                                      class_of[:, bass.ds(b0, G)].unsqueeze(2).to_broadcast([P, G, NCLASS]), ALU.is_equal))
                own.sync()
                own(dve.tensor_tensor(pick[:, 1], pick[:, 0], offset.unsqueeze(1).to_broadcast([P, G, NCLASS]), ALU.mult))
                own.sync()
                own(dve.tensor_reduce(place[:, s, :], pick[:, 1], AX_X, ALU.add))
                own.sync()
                own(dve.tensor_tensor(place_i[:, 0, s, :], place[:, s, :], rank_of[:, bass.ds(b0, G)], ALU.add))
                own.sync()
                own(dve.tensor_scalar(place_i[:, 1, s, :], place_i[:, 0, s, :], P - 1, None, ALU.bitwise_and))
                own(dve.tensor_scalar(place_i[:, 2, s, :], place_i[:, 0, s, :], P.bit_length() - 1, None, ALU.logical_shift_right))
                own.sync()
                wait_turn(dve, s_inv, 1, t, -1)
                wait_turn(dve, s_hot_n, 1, t, -1)
                wait_turn(dve, s_hot_b, 1, t, -1)
                dve.tensor_tensor(at_row[:, s], iota_b[:, 0:P].unsqueeze(1).to_broadcast([P, G, P]),
                                  place_i[:, 1, s, :].unsqueeze(2).to_broadcast([P, G, P]), ALU.is_equal).then_inc(s_hot, 1)
                dve.tensor_tensor(at_col[:, s], iota_b[:, 0:COLS].unsqueeze(1).to_broadcast([P, G, COLS]),
                                  place_i[:, 2, s, :].unsqueeze(2).to_broadcast([P, G, COLS]), ALU.is_equal).then_inc(s_hot_c, 1)

            for k in range(2):
                n0 = own.n
                one_hots(Turn(0, k, 2, CHUNKS), k * G)
                own_each = own.n - n0
            with dve.Fori(1, CHUNKS // 2) as g:
                own.enter(g, 1, 2 * own_each)
                for k in range(2):
                    t = Turn(g, k, 2, CHUNKS)
                    one_hots(t, t.index * G)
                own.leave(CHUNKS // 2 - 1)

            dve.wait_ge(s_inv, CHUNKS + 1)
            node, graph, empty, target = (inv[:, i, :] for i in range(4))
            own(dve.tensor_copy(node, ps_a))
            own(dve.tensor_copy(graph, ps_b))
            own.sync()
            shaped = lambda a: a.rearrange("p (t j) -> p t j", j=BLK)
            own(dve.scalar_tensor_tensor(out=index[:, :, 0:BLK], in0=shaped(node), scalar=float(NB), in1=shaped(graph), op0=ALU.mult, op1=ALU.add))
            own(dve.tensor_scalar(empty, graph, 0.0, 4.0 * TOKENS, ALU.is_equal, ALU.mult))
            own(dve.scalar_tensor_tensor(out=target, in0=graph, scalar=float(N), in1=node, op0=ALU.mult, op1=ALU.add))
            own.sync()
            dve.scalar_tensor_tensor(out=index[:, :, BLK:2 * BLK], in0=shaped(target), scalar=-float(N), in1=shaped(empty),
                                     op0=ALU.add, op1=ALU.add).then_inc(s_index, 1)

            def tile_lo(t):
                wait_turn(dve, s_inhi, 1, t, 1)
                k = t.slot(2)
                dve.tensor_tensor(in_lo[:, k], ps_x, in_hi[:, k].bitcast(F32), ALU.subtract).then_inc(s_inlo, 1)

            def split(t, s):
                wait_turn(dve, s_mm2[s], 1, t, 0)
                for k in range(2):
                    cs = slice(k * FC // 2, (k + 1) * FC // 2)
                    wait_turn(dve, s_act[s], FC, t, (k + 1) * FC // 2)
                    dve.tensor_copy(act_hi[:, s, cs, :], act_f[:, s, cs, :]).then_inc(s_hhi, 1)
                    wait_turn(dve, s_hhi, 4, t, 2 * s + k + 1)
                    dve.tensor_tensor(act_lo[:, s, cs, :], act_f[:, s, cs, :], act_hi[:, s, cs, :].bitcast(F32),
                                      ALU.subtract).then_inc(s_split[s], 1)

            def sum_up(t):
                if t.real:
                    i = t.slot(UT)
                    wait_turn(dve, s_o, 1, t, 1)
                    for j in range(BLK):
                        last = dve.scalar_tensor_tensor(out=y_one[:, j, :], in0=ps_o[:, 0, j, :], scalar=got[:, i, j, 2 * P:2 * P + 1],
                                                        in1=got[:, i, j, P:2 * P], op0=ALU.mult, op1=ALU.add)
                    last.then_inc(s_y1, 1)
                    wait_turn(dve, s_y1, 1, t, 1)
                    wait_slot(dve, s_out, 16 * BLK, t, 0)
                    for j in range(BLK):
                        last = dve.scalar_tensor_tensor(out=y_out[:, i, j, :], in0=ps_o[:, 1, j, :], scalar=got[:, i, j, 2 * P + 1:2 * P + 2],
                                                        in1=y_one[:, j, :], op0=ALU.mult, op1=ALU.add)
                    last.then_inc(s_done[i], 1)

            def tile(t):
                split(t, 0)
                tile_lo(Turn(t.group, t.step + 1, UT, NT))
                split(t, 1)
                sum_up(t.back(1))

            tile_lo(Turn(0, 0, UT, NT))
            every_turn(dve, UT, NT, tile)
            sum_up(END.back(1))

        @block.tensor
        def _(pe):
            pe.wait_ge(s_const, N_CONST)
            pe.wait_ge(s_small, 16 * 10)
            pe.transpose(ps_t[:, 0, 0, :], adj_s[:], ident[:]).then_inc(s_adjt, 1)
            pe.wait_ge(s_adj, 5)

            def transposed(t, src, s_src, s_dst, free):
                if t.real:
                    wait_turn(pe, s_src, 1, t, 1)
                    for sem_, each, turn, more in free:
                        wait_turn(pe, sem_, each, turn, more)
                    for b in range(G):
                        last = pe.transpose(ps_t[:, b // 4, b % 4, :], src(b), ident[:])
                        if b % 4 == 3:
                            last.then_inc(s_dst, 1)

            def products(t):
                if t.real:
                    wait_turn(pe, s_tin, 1, t, 0)
                    wait_turn(pe, s_comb, 1, t, 0)
                    for k in range(2):
                        rhs = hs[:, t.slot(2), 4 * k:4 * k + 4, :]
                        for dst, w, e in ((ps_in, adj_in, 0), (ps_out, adj_out, 1)):
                            pe.matmul(dst[:, k], w[:], rhs, start=True, stop=False)
                            pe.matmul(dst[:, k], ident_r[:], eb_hi[:, e], start=False, stop=False)
                            last = pe.matmul(dst[:, k], ident_r[:], eb_lo[:, e], start=False, stop=True)
                    last.then_inc(s_prod, 1)

            def small(t, s_src, src, w, dst, s_free, s_dst):
                if t.real:
                    wait_turn(pe, s_src, 2, t, 2)
                    wait_turn(pe, s_free, 1, t, 0)
                    for b in range(G):
                        last = pe.matmul(dst(b), src[:, b, :], w[:], start=True, stop=True)
                    last.then_inc(s_dst, 1)

            def chunk(t):
                b2_ = t.back(2)
                first = (s_ht, 2, t, 0) if t.real else (s_ht, 2, Turn(0, CHUNKS, CHUNKS, CHUNKS), 0)
                transposed(b2_, lambda b: row[:, b2_.slot(2), b, 0:P], s_h2, s_h2t_ps, [first, (s_h2t, 2, b2_, 0)])
                small(b2_, s_h2t, h2T, wg_s, lambda b: ps_logit[:, b, :], s_lsum, s_logit)
                transposed(t, lambda b: hs[:, t.slot(2), b, :], s_h, s_ht_ps, [(s_ht, 2, t, 0), (s_h2t, 2, b2_, 2)])
                products(t)
                small(t, s_ht, hT, gate_w, lambda b: ps_gate[:, b, 0:3], s_sig, s_gate)

            for k in range(UA):
                chunk(Turn(0, k, UA, CHUNKS))
            with pe.Fori(1, CHUNKS // UA) as g:
                for k in range(UA):
                    chunk(Turn(g, k, UA, CHUNKS))
            for k in range(2):
                chunk(Turn(CHUNKS // UA, k, UA, CHUNKS))

            pe.wait_ge(s_tot, 1)
            pe.matmul(ps_pre, before[:], totals[:], start=True, stop=True)
            pe.matmul(ps_tot, ones_b[:], totals[:], start=True, stop=True).then_inc(s_tot_ps, 1)

            pe.wait_ge(s_rep, 1)
            pe.wait_ge(s_bias, 32)
            for s in range(2):
                last = pe.matmul(ps_exp[:, s, :], expert_rep[:, s, :], ident[:], start=True, stop=True)
            last.then_inc(s_exp_ps, 1)
            pe.wait_ge(s_exp_hot, 1)
            for c in range(FC):
                pe.matmul(ps_bias[:, c], b1_s[:, c * P:(c + 1) * P], expert_hot[:], start=True, stop=True)
            last = pe.matmul(ps_bias[:, FC], b2_s[:], expert_hot[:], start=True, stop=True)
            last.then_inc(s_b_ps, 1)

            def inverse(t):
                wait_turn(pe, s_hot_n, 1, t, 1)
                wait_turn(pe, s_hot_b, 1, t, 1)
                s = t.slot(2)
                wait_turn(pe, s_hot_c, 1, t, 1)
                for b in range(G):
                    pe.matmul(ps_a, at_row_n[:, s, b, :], at_col[:, s, b, :], start=False, stop=False)
                    last = pe.matmul(ps_b, at_row_b[:, s, b, :], at_col[:, s, b, :], start=False, stop=False)
                last.then_inc(s_inv, 1)

            for dst in (ps_a, ps_b):
                pe.matmul(dst, zeros_b[:, 0:P], zeros_b[:], start=True, stop=False)
            for k in range(2):
                inverse(Turn(0, k, 2, CHUNKS))
            with pe.Fori(1, CHUNKS // 2) as g:
                for k in range(2):
                    inverse(Turn(g, k, 2, CHUNKS))
            for dst in (ps_a, ps_b):
                last = pe.matmul(dst, zeros_b[:, 0:P], zeros_b[:], start=False, stop=True)
            last.then_inc(s_inv, 1)

            pe.wait_ge(s_btab, 1)

            def tile_in(t):
                s = t.slot(UT)
                wait_slot(pe, s_got, 16 * BLK, t, 16 * BLK)
                wait_turn(pe, s_inlo, 1, t, 0)
                for j in range(BLK):
                    last = pe.transpose(ps_x[:, j * P:(j + 1) * P], got[:, s, j, 0:P], ident[:])
                last.then_inc(s_xt, 1)

            def layer1(t, s):
                k = t.slot(2)
                wait_turn(pe, s_wt[0][s], 16, t, 16)
                wait_turn(pe, s_inlo, 1, t, 1)
                wait_turn(pe, s_inhi, 1, t, 1)
                wait_turn(pe, s_act[s], FC, t, 0)
                for c in range(FC):
                    hi = wt[0][:, s, c * P:(c + 1) * P]
                    lo = wt[0][:, s, H + c * P:H + (c + 1) * P]
                    pe.matmul(ps_h[s][:, c, :], hi, in_hi[:, k], start=True, stop=False)
                    pe.matmul(ps_h[s][:, c, :], hi, in_lo[:, k], start=False, stop=False)
                    last = pe.matmul(ps_h[s][:, c, :], lo, in_hi[:, k], start=False, stop=True)
                    if c % 2:
                        last.then_inc(s_mm1[s], 1)

            def layer2(t, s):
                if t.real:
                    wait_turn(pe, s_wt[1][s], 16, t, 16)
                    wait_turn(pe, s_y[s], 1, t, 0)
                    for c in range(FC):
                        if c % 2 == 0:
                            wait_turn(pe, s_split[s], 2, t, c // 2 + 1)
                        hi = wt[1][:, s, c * P:(c + 1) * P]
                        lo = wt[1][:, s, H + c * P:H + (c + 1) * P]
                        pe.matmul(ps_y[s], hi, act_hi[:, s, c, :], start=(c == 0), stop=False)
                        pe.matmul(ps_y[s], hi, act_lo[:, s, c, :], start=False, stop=False)
                        last = pe.matmul(ps_y[s], lo, act_hi[:, s, c, :], start=False, stop=(c == FC - 1))
                    last.then_inc(s_mm2[s], 1)

            def tile_out(t):
                if t.real:
                    for s in range(2):
                        wait_turn(pe, s_y[s], 1, t, 1)
                    wait_slot(pe, s_done, 1, t.back(1), 1)
                    for s in range(2):
                        for j in range(BLK):
                            last = pe.transpose(ps_o[:, s, j, :], y_t[:, s, j * P:(j + 1) * P], ident[:])
                    last.then_inc(s_o, 1)

            def tile(t):
                layer1(t, 0)
                layer2(t.back(1), 1)
                tile_in(Turn(t.group, t.step + 1, UT, NT))
                layer1(t, 1)
                tile_out(t.back(1))
                layer2(t, 0)

            tile_in(Turn(0, 0, UT, NT))
            every_turn(pe, UT, NT, tile)
            layer2(END.back(1), 1)
            tile_out(END.back(1))


_INS = ["x", "adj", "L0_gnn_edge_bias", "L0_gnn_gate_weight", "L0_gnn_bias_gate", "L0_gnn_out_edge_bias",
        "L0_gnn_out_gate_weight", "L0_gnn_out_bias_gate", "L0_gnn_loop_gate", "L0_ffn_Wg", "L0_ffn_bg",
        "L0_ffn_W1", "L0_ffn_b1", "L0_ffn_W2", "L0_ffn_b2"]


def kernel(**inputs):
    import numpy as _np
    import concourse.bacc as _bacc
    from concourse import mybir as _mybir
    from concourse.bass_utils import run_bass_kernel_spmd as _run

    nc = _bacc.Bacc("TRN2", target_bir_lowering=False, num_devices=1)
    arrays, args = {}, []
    for name in _INS:
        a = _np.ascontiguousarray(inputs[name])
        arrays[f"in_{name}_dram"] = a
        args.append(nc.dram_tensor(f"in_{name}_dram", a.shape, _mybir.dt.from_np(a.dtype), kind="ExternalInput").ap())
    shape = inputs["x"].shape
    args.append(nc.dram_tensor("out_0_dram", shape, _mybir.dt.float32, kind="ExternalOutput").ap())
    program(nc, *args)
    r = _run(nc, [arrays], core_ids=[0])
    return r.results[0]["out_0_dram"]
```

```python
from contextlib import ExitStack

import concourse.bass as bass
from concourse import mybir

F32 = mybir.dt.float32
F32R = mybir.dt.float32r
BF16 = mybir.dt.bfloat16
I32 = mybir.dt.int32
U32 = mybir.dt.uint32
ALU = mybir.AluOpType
ACT = mybir.ActivationFunctionType
AX_X = mybir.AxisListType.X

P = 128
G = 8
E = 8
EPS = 1e-5
RSQRT_SEED = float(0x5F3759DF)
FIRST = [(a, b) for a in range(E) for b in range(a + 1, E)]
NCLASS = len(FIRST)
TILE = 256
BLK = TILE // P
ROW = 2 * P + 4


class Turn:

    def __init__(self, group, step, unroll, total):
        self.group, self.step, self.unroll, self.total = group, step, unroll, total
        self.index = group * unroll + step

    def back(self, n):
        return Turn(self.group, self.step - n, self.unroll, self.total)

    def slot(self, ring):
        assert self.unroll % ring == 0
        return self.step % ring

    @property
    def real(self):
        return not isinstance(self.index, int) or 0 <= self.index < self.total


def wait_turn(eng, sem, each, turn, more):
    value = turn.group * (each * turn.unroll) + (each * turn.step + more)
    if not isinstance(value, int) or value > 0:
        eng.wait_ge(sem, value)


def wait_slot(eng, sems, each, turn, more):
    ring = len(sems)
    s = turn.slot(ring)
    wait_turn(eng, sems[s], each, Turn(turn.group, (turn.step - s) // ring, turn.unroll // ring, 0), more)


def apart(eng, sem):
    eng.wait_ge(sem, 1)


def every_turn(eng, unroll, total, body, until=None, first=1, own=None, last=None):
    until = total if until is None else until
    last = until // unroll if last is None else last
    for k in range(first * unroll):
        before = own.n if own else 0
        body(Turn(k // unroll, k % unroll, unroll, total))
        each = own.n - before if own else 0
    with eng.Fori(first, last) as g:
        if own:
            own.enter(g, first, unroll * each)
        for k in range(unroll):
            body(Turn(g, k, unroll, total))
        if own:
            own.leave(last - first)
    for k in range(last * unroll, until):
        body(Turn(k // unroll, k % unroll, unroll, total))


class Own:

    def __init__(self, eng, sem):
        self.eng, self.sem, self.base, self.n = eng, sem, 0, 0

    def __call__(self, ins):
        ins.then_inc(self.sem, 1)
        self.n += 1

    def sync(self):
        self.eng.wait_ge(self.sem, self.base + self.n)

    def enter(self, group, first, each):
        self.start, self.each = self.n, each
        self.base = (group * each) + (self.n - first * each)
        self.n = 0

    def leave(self, rounds):
        assert self.n == self.each, (self.n, self.each)
        self.base, self.n = 0, self.start + rounds * self.each


def program(nc, x, adj, edge_bias, gate_weight, bias_gate, out_edge_bias, out_gate_weight,
            out_bias_gate, loop_gate, Wg, bg, W1, b1, W2, b2, out):
    NB, N, D = x.shape
    H = W1.shape[2]
    assert N == P and D == P and NB % (4 * G) == 0 and W1.shape[0] == E
    FC = H // P
    CHUNKS = NB // G
    TOKENS = NB * N
    NT = TOKENS // TILE + NCLASS - 1
    NTG = NT + 1
    COLS = NTG * BLK
    UA, UT = 4, 4
    END = Turn(NT // UT, NT % UT, UT, NT)
    assert CHUNKS % UA == 0
    GRAPH_LOOP = dict(until=CHUNKS + 6, first=2, last=CHUNKS // UA)

    w_dram = [nc.dram_tensor(f"w{l}_split", (16, P, 2 * H), F32).ap() for l in (1, 2)]
    rows = nc.dram_tensor("rows", (TOKENS + 1, ROW), F32).ap()
    rows_by_node = rows[1:TOKENS + 1, :].rearrange("(n b) k -> n b k", n=N)
    experts_dram = nc.dram_tensor("tile_experts", (NTG, 1), I32).ap()
    x_by_node = x.rearrange("b n d -> n b d")
    out_rows = out.rearrange("b n d -> (b n) d")

    with ExitStack() as ctx:
        def sb(name, shape, dt=F32):
            return ctx.enter_context(nc.sbuf_tensor(name, list(shape), dt))

        def sem(name):
            return ctx.enter_context(nc.semaphore(name))

        bank = ctx.enter_context(nc.psum_tensor("bank", [P, 8, 512], F32))

        ident = sb("ident", [P, P])
        ident_r = sb("ident_r", [P, P], F32R)
        ones_f = sb("ones_f", [P, P])
        before = sb("before", [P, P], BF16)
        ones_b = sb("ones_b", [P, P], BF16)
        zeros_b = sb("zeros_b", [P, COLS], BF16)
        iota_i = sb("iota_i", [P, 256], I32)
        iota_f = sb("iota_f", [P, 256])
        iota_b = sb("iota_b", [P, 256], BF16)
        graph_b = sb("graph_b", [P, NB], BF16)
        node_i = sb("node_i", [P, 1], I32)
        node_f = sb("node_f", [P, 1])
        step_e = sb("step_e", [P, 2, NCLASS])
        keep = sb("keep", [P, NCLASS, G + 1])
        adj_s = sb("adj_s", [P, P])
        adj_t = sb("adj_t", [P, P])
        tmp_m = sb("tmp_m", [P, 2, P])
        adj_in = sb("adj_in", [P, P])
        adj_out = sb("adj_out", [P, P])
        eb = sb("eb", [P, 2, P])
        eb_hi = sb("eb_hi", [P, 2, 4, P], F32R)
        eb_lo = sb("eb_lo", [P, 2, 4, P], F32R)
        gate_w = sb("gate_w", [P, 3])
        gate_b = sb("gate_b", [P, 2])
        wg_s = sb("wg_s", [P, E])
        bg_s = sb("bg_s", [P, E])
        xs = sb("xs", [P, 4, G, D])
        hs = sb("hs", [P, 2, G, D])
        row = sb("row", [P, 4, G, ROW])
        hT = sb("hT", [P, G, P])
        h2T = sb("h2T", [P, G, P])
        t_in = sb("t_in", [P, G, D])
        t_loop = sb("t_loop", [P, G, D])
        t_sum = sb("t_sum", [P, G, D])
        sig = sb("sig", [P, 2, 3, G])
        stats = sb("stats", [P, 2, G, 6])
        ln_tmp = sb("ln_tmp", [P, 8, 2, G])
        ln_bits = sb("ln_bits", [P, 2, 2, G], I32)
        rstd = sb("rstd", [P, 2, G])
        shift = sb("shift", [P, 2, G])
        logit = sb("logit", [P, G, E])
        top = sb("top", [P, G, 8])
        top_at = sb("top_at", [P, G, 8], U32)
        rt = sb("rt", [P, 8, G])
        margin = sb("margin", [P, G])
        hot = sb("hot", [P, NCLASS, G + 1])
        count = sb("count", [P, NCLASS, G + 1])
        ranked = sb("ranked", [P, NCLASS, G])
        class_of = sb("class_of", [P, NB])
        rank_of = sb("rank_of", [P, NB])
        totals = sb("totals", [P, NCLASS], BF16)
        pl = sb("pl", [P, 6, NCLASS])
        pl_i = sb("pl_i", [P, 2, NCLASS], I32)
        pick = sb("pick", [P, 2, G, NCLASS])
        place = sb("place", [P, 2, G])
        place_i = sb("place_i", [P, 3, 2, G], I32)
        at_row = sb("at_row", [P, 2, G, P], BF16)
        at_row_n = sb("at_row_n", [P, 2, G, P], BF16)
        at_row_b = sb("at_row_b", [P, 2, G, P], BF16)
        at_col = sb("at_col", [P, 2, G, COLS], BF16)
        inv = sb("inv", [P, 4, COLS])
        index = sb("index", [P, NTG, 2 * BLK], I32)
        started = sb("started", [P, 2, NCLASS])
        steps = sb("steps", [P, 4, NCLASS])
        node_b = sb("node_b", [P, 2])
        expert = sb("expert", [P, 4])
        change = sb("change", [P, 3, 2])
        code = sb("code", [P, 1], I32)
        expert_rep = sb("expert_rep", [P, 2, E])
        expert_hot = sb("expert_hot", [E, 2, P])
        b_of_tile = sb("b_of_tile", [P, FC + 1, 2, P])
        zero_row = sb("zero_row", [1, ROW])
        w_in = sb("w_in", [P, 2, 2, H])
        w_split = sb("w_split", [P, 2, 2, 2, H], F32R)
        b1_s = sb("b1_s", [E, H])
        b2_s = sb("b2_s", [E, D])
        wt = [sb(f"wt{l}", [P, 2, 2 * H], F32R) for l in (1, 2)]
        b_t = sb("b_t", [P, UT, FC + 1, 2])
        from_row = sb("from_row", [P, UT, BLK], I32)
        to_row = sb("to_row", [P, UT, BLK], I32)
        got = sb("got", [P, UT, BLK, ROW])
        in_hi = sb("in_hi", [P, 2, TILE], F32R)
        in_lo = sb("in_lo", [P, 2, TILE], F32R)
        act_f = w_in[:].rearrange("p s a (b m) -> p s (a b) m", m=TILE)
        act_hi, act_lo = (w_split[:, i].rearrange("p s a (b m) -> p s (a b) m", m=TILE) for i in range(2))
        y_t = sb("y_t", [P, 2, TILE])
        y_one = sb("y_one", [P, BLK, D])
        y_out = sb("y_out", [P, UT, BLK, D])

        ps_t = bank[:, 0:2, :].rearrange("p k (g m) -> p k g m", g=4)
        ps_in = bank[:, 2:4, :].rearrange("p k (g m) -> p k g m", g=4)
        ps_out = bank[:, 4:6, :].rearrange("p k (g m) -> p k g m", g=4)
        ps_gate = bank[:, 6, 0:4 * G].rearrange("p (g k) -> p g k", k=4)
        ps_logit = bank[:, 7, 64:64 + G * E].rearrange("p (g e) -> p g e", e=E)
        ps_pre = bank[:, 7, 0:NCLASS]
        ps_tot = bank[:, 7, 64:64 + NCLASS]
        ps_a = bank[:, 0, 0:COLS]
        ps_b = bank[:, 1, 0:COLS]
        ps_h = [bank[:, 2 * s:2 * s + 2, :].rearrange("p k (c m) -> p (k c) m", m=TILE) for s in range(2)]
        ps_y = [bank[:, 4 + s, 0:TILE] for s in range(2)]
        ps_x = bank[:, 6, 0:TILE]
        ps_o = bank[:, 7, :].rearrange("p (s j m) -> p s j m", s=2, j=BLK)
        ps_exp = bank[0:E, 2, 0:2 * P].rearrange("p (s t) -> p s t", s=2)
        ps_bias = bank[:, 4:7, :].rearrange("p k (c s t) -> p (k c) s t", s=2, t=P)[:, 0:FC + 1]

        s_const = sem("pool_constants")
        s_iota = sem("iota_copies")
        s_small = sem("small_inputs_loaded")
        s_bias = sem("biases_loaded")
        s_adjt = sem("adj_transposed")
        s_adj = sem("adj_matrices_ready")
        s_x = [sem(f"x_loaded{i}") for i in range(4)]
        s_norms = sem("norms_ready")
        s_h = sem("h_ready")
        s_ht_ps = sem("hT_in_psum")
        s_ht = sem("hT_copied")
        s_gate = sem("gates_in_psum")
        s_prod = sem("products_in_psum")
        s_sig = sem("sigmoids_ready")
        s_tloop = sem("t_loop_ready")
        s_tin = sem("t_in_ready")
        s_tout = sem("t_out_added")
        s_tsum = sem("t_sum_ready")
        s_x1 = sem("x1_ready")
        s_h2 = sem("h2_ready")
        s_h2t_ps = sem("h2T_in_psum")
        s_h2t = sem("h2T_copied")
        s_logit = sem("logits_in_psum")
        s_lsum = sem("logits_read")
        s_margin = sem("margins_ready")
        s_rw = sem("row_weights_ready")
        s_row = [sem(f"row_stored{i}") for i in range(4)]
        s_dve = sem("dve_own")
        s_pool = sem("pool_own")
        s_tot = sem("totals_ready")
        s_tot_ps = sem("totals_in_psum")
        s_hot = sem("one_hots_ready")
        s_hot_c = sem("column_hots_ready")
        s_hot_n = sem("row_hots_times_node")
        s_hot_b = sem("row_hots_times_graph")
        s_inv = sem("inverse_products")
        s_index = sem("index_ready")
        s_texp = sem("tile_experts_ready")
        s_tab = sem("tile_experts_stored")
        s_wl = [sem(f"w_staged{i}") for i in range(2)]
        s_whi = sem("w_hi_ready")
        s_wlo = sem("w_lo_ready")
        s_ws = [sem(f"w_split_stored{i}") for i in range(2)]
        s_bs = sem("zero_row_stored")
        s_rep = sem("tile_experts_repeated")
        s_exp_ps = sem("tile_experts_on_all_partitions")
        s_exp_hot = sem("tile_experts_one_hot")
        s_b_ps = sem("b_of_tiles_in_psum")
        s_btab = sem("b_of_tiles_copied")
        s_wt = [[sem(f"w{l}_of_slot{s}") for s in range(2)] for l in (1, 2)]
        s_first = sem("first_gather_indices_copied")
        s_from = [sem(f"gather_index_copied{i}") for i in range(UT)]
        s_to = [sem(f"scatter_index_copied{i}") for i in range(UT)]
        s_got = [sem(f"rows_gathered{i}") for i in range(UT)]
        s_xt = sem("tile_transposed")
        s_inhi = sem("tile_hi")
        s_inlo = sem("tile_lo")
        s_mm1 = [sem(f"hidden_in_psum{s}") for s in range(2)]
        s_act = [sem(f"gelu_done{s}") for s in range(2)]
        s_hhi = sem("hidden_hi")
        s_split = [sem(f"hidden_split{s}") for s in range(2)]
        s_mm2 = [sem(f"expert_out_in_psum{s}") for s in range(2)]
        s_y = [sem(f"expert_out_copied{s}") for s in range(2)]
        s_o = sem("outputs_transposed")
        s_bt = [sem(f"tile_b1_copied{i}") for i in range(UT)]
        s_y1 = sem("first_expert_added")
        s_done = [sem(f"tile_summed{i}") for i in range(UT)]
        s_out = [sem(f"rows_scattered{i}") for i in range(UT)]
        N_CONST = 14

        block = ctx.enter_context(nc.Block())

        @block.sync
        def _(sp):
            sp.dma_start(adj_s[:], adj).then_inc(s_small, 16)
            sp.dma_start(eb[:, 0, :], edge_bias).then_inc(s_small, 16)
            sp.dma_start(eb[:, 1, :], out_edge_bias).then_inc(s_small, 16)

            def load_x(t):
                if t.real:
                    wait_turn(sp, s_x1, 1, t.back(4), 1)
                    b = t.index * G
                    sp.dma_start(xs[:, t.slot(4)], x_by_node[:, bass.ds(b, G), :]).then_inc(s_x[t.slot(4)], 16)

            for k in range(UA):
                load_x(Turn(0, k, UA, CHUNKS))
            for k, w in enumerate((gate_weight, out_gate_weight, loop_gate)):
                sp.dma_start(gate_w[:, k:k + 1], w).then_inc(s_small, 16)
            sp.dma_start(gate_b[:, 0:1], bias_gate).then_inc(s_small, 16)
            sp.dma_start(gate_b[:, 1:2], out_bias_gate).then_inc(s_small, 16)
            sp.dma_start(wg_s[:], Wg).then_inc(s_small, 16)
            sp.dma_start(bg_s[:], bg.partition_broadcast(P)).then_inc(s_small, 16)
            sp.dma_start(b1_s[:], b1).then_inc(s_bias, 16)
            sp.dma_start(b2_s[:], b2).then_inc(s_bias, 16)

            def w_source(k):
                layer, e = k // (E // 2), 2 * (k % (E // 2))
                if layer == 0:
                    return W1[e:e + 2].rearrange("e p h -> p e h")
                return W2[e:e + 2].rearrange("e (c p) d -> p e c d", p=P)

            def load_w(k):
                if k >= 2:
                    sp.wait_ge(s_wlo, k - 1)
                dst = w_in[:, k % 2]
                if k >= E // 2:
                    dst = dst.rearrange("p e (c d) -> p e c d", c=FC)
                src = w_source(k)
                for e in range(2):
                    sp.dma_start(dst[:, e], src[:, e]).then_inc(s_wl[k % 2], 16)

            def store_w(k):
                layer, e = k // (E // 2), 2 * (k % (E // 2))
                sp.wait_ge(s_wlo, k + 1)
                dst = w_dram[layer][e:e + 2].rearrange("e p h -> p e h")
                sp.dma_start(dst, w_split[:, k % 2].bitcast(F32).rearrange("p e k h -> p e (k h)")).then_inc(s_ws[k % 2], 16)

            load_w(0)
            load_w(1)

            for w in range(E):
                store_w(w)
                if w + 2 < E:
                    load_w(w + 2)
            sp.wait_ge(s_const, N_CONST)
            sp.dma_start(rows[0:1, :], zero_row[:]).then_inc(s_bs, 16)
            with sp.Fori(1, CHUNKS // UA) as g:
                for k in range(UA):
                    load_x(Turn(g, k, UA, CHUNKS))

            sp.wait_ge(s_texp, 1)
            sp.dma_start(experts_dram, code[0:NTG, :]).then_inc(s_tab, 16)
            sp.wait_ge(s_tab, 16)
            for i in range(2):
                sp.wait_ge(s_ws[i], 16 * E // 2)
            sp.wait_ge(s_bs, 16)

            def codes(t):
                both = sp.value_load(experts_dram[bass.ds(t.index, 1), :], min_val=0, max_val=16 * E + E)
                return [sp.snap(both >> 4, min_val=0, max_val=E), sp.snap(both & 15, min_val=0, max_val=E)]

            def load_slot(l, s, new, t, used, each):
                with sp.If_ne(sp.to_reg(new[s]), E):
                    wait_turn(sp, used[s], each, t, 0)
                    sp.dma_start(wt[l][:, s, :].bitcast(F32), w_dram[l][bass.ds(new[s], 1)].rearrange("a p h -> (a p) h")).then_inc(s_wt[l][s], 16)
                with sp.Else():
                    wait_turn(sp, used[s], each, t, 0)
                    sp.sem_inc(s_wt[l][s], 16)

            ahead = []

            def weights(t):
                new = ahead.pop() if t.step % UT else codes(t)
                load_slot(0, 0, new, t, s_mm1, 2)
                load_slot(0, 1, new, t, s_mm1, 2)
                load_slot(1, 0, new, t, s_mm2, 1)
                if t.step % UT < UT - 1:
                    ahead.append(codes(Turn(t.group, t.step + 1, UT, NT)))
                load_slot(1, 1, new, t, s_mm2, 1)

            every_turn(sp, UT, NT, weights)
            for i in range(UT):
                sp.wait_ge(s_out[i], 16 * BLK * ((NT + UT - 1 - i) // UT))

        @block.gpsimd
        def _(pool):
            own = Own(pool, s_pool)
            pool.memset(ones_f[:], 1.0).then_inc(s_const, 1)
            pool.memset(ident[:], 0.0).then_inc(s_const, 1)
            pool.memset(ones_b[:], 1.0).then_inc(s_const, 1)
            pool.memset(zeros_b[:], 0.0).then_inc(s_const, 1)
            pool.memset(keep[:], 1.0).then_inc(s_const, 1)
            pool.memset(step_e[:, 0, :], 0.0).then_inc(s_const, 1)
            pool.memset(step_e[:, 1, :], 1.0).then_inc(s_const, 1)
            pool.memset(zero_row[:], 0.0).then_inc(s_const, 1)
            pool.iota(iota_i[:], pattern=[[1, 256]], base=0, channel_multiplier=0).then_inc(s_const, 1)
            pool.iota(node_i[:], pattern=[[0, 1]], base=0, channel_multiplier=1).then_inc(s_const, 1)
            pool.wait_ge(s_const, 10)
            pool.affine_select(out=ident[:], in_=ident[:], pattern=[[-1, P]], compare_op=ALU.not_equal,
                               fill=1.0, base=0, channel_multiplier=1).then_inc(s_const, 1)
            pool.affine_select(out=before[:], in_=ones_b[:], pattern=[[1, P]], compare_op=ALU.is_gt,
                               fill=0.0, base=0, channel_multiplier=-1).then_inc(s_const, 1)
            pool.memset(keep[:, :, 0:1], 0.0).then_inc(s_const, 1)
            for c in range(1, NCLASS):
                for s in range(2):
                    d = FIRST[c][s] - FIRST[c - 1][s]
                    if d != s:
                        own(pool.memset(step_e[:, s, c:c + 1], float(d)))
            own.sync()
            pool.memset(row[:, :, :, 2 * P + 2:ROW], 0.0).then_inc(s_const, 1)

            def mix(t):
                if t.real:
                    wait_turn(pool, s_sig, 1, t, 1)
                    wait_turn(pool, s_tout, 2, t, 0)
                    gate = sig[:, t.slot(2), 2, :].unsqueeze(2).to_broadcast([P, G, D])
                    pool.tensor_tensor(t_loop[:], hs[:, t.slot(2)], gate, ALU.mult).then_inc(s_tloop, 1)
                    wait_turn(pool, s_tin, 2, t, 2)
                    wait_turn(pool, s_tout, 2, t, 2)
                    pool.tensor_tensor(t_sum[:], t_sum[:], t_in[:], ALU.add).then_inc(s_tsum, 1)

            def split_lo(k):
                pool.wait_ge(s_whi, k + 1)
                for e in range(2):
                    last = pool.tensor_tensor(w_split[:, k % 2, e, 1], w_in[:, k % 2, e],
                                              w_split[:, k % 2, e, 0].bitcast(F32), ALU.subtract)
                last.then_inc(s_wlo, 1)

            def turn(t):
                if isinstance(t.index, int) and t.index < E // 2:
                    for w in (2 * t.index, 2 * t.index + 1):
                        if w >= 2:
                            pool.wait_ge(s_ws[w % 2], 16 * (w // 2))
                        split_lo(w)
                mix(t.back(2))

            every_turn(pool, UA, CHUNKS, turn, **GRAPH_LOOP)

            def times_graph(t, b):
                wait_turn(pool, s_hot, 1, t, 1)
                wait_turn(pool, s_inv, 1, t, -1)
                pool.tensor_tensor(at_row_b[:, t.slot(2)], at_row[:, t.slot(2)],
                                   graph_b[:, bass.ds(b, G)].unsqueeze(2).to_broadcast([P, G, P]),
                                   ALU.mult).then_inc(s_hot_b, 1)

            pool.wait_ge(s_iota, 6)
            for k in range(2):
                times_graph(Turn(0, k, 2, CHUNKS), k * G)
            with pool.Fori(1, CHUNKS // 2) as g:
                for k in range(2):
                    t = Turn(g, k, 2, CHUNKS)
                    times_graph(t, t.index * G)

            pool.wait_ge(s_index, 1)
            pool.wait_ge(s_btab, 1)
            pool.wait_ge(s_bs, 16)
            for i in range(4):
                pool.wait_ge(s_row[i], 16 * CHUNKS // 4)

            def gather(t, copied):
                s = t.slot(UT)
                wait_slot(pool, s_done, 1, t.back(UT), 1)
                wait_slot(pool, s_got, 16 * BLK, t, 0)
                pool.tensor_copy(from_row[:, s, :], index[:, bass.ds(t.index, 1), 0:BLK].rearrange("p a k -> p (a k)")).then_inc(copied, 1)
                pool.tensor_copy(b_t[:, s], b_of_tile[:, :, :, bass.ds(t.index, 1)].rearrange("p c s a -> p c (s a)")).then_inc(s_bt[s], 1)
                apart(pool, s_const)
                if copied is s_first:
                    pool.wait_ge(s_first, t.index + 1)
                else:
                    wait_slot(pool, s_from, 1, t.back(UT), 1)
                for j in range(BLK):
                    pool.indirect_dma_start(out=got[:, s, j, :], out_offset=None, in_=rows,
                                            in_offset=bass.IndirectOffsetOnAxis(ap=from_row[:, s, j:j + 1], axis=0)).then_inc(s_got[s], 16)

            def scatter(t):
                s = t.slot(UT)
                wait_slot(pool, s_done, 1, t, 1)
                wait_slot(pool, s_out, 16 * BLK, t, 0)
                pool.tensor_copy(to_row[:, s, :], index[:, bass.ds(t.index, 1), BLK:2 * BLK].rearrange("p a k -> p (a k)")).then_inc(s_to[s], 1)
                apart(pool, s_const)
                wait_slot(pool, s_to, 1, t, 1)
                for j in range(BLK):
                    pool.indirect_dma_start(out=out_rows, out_offset=bass.IndirectOffsetOnAxis(ap=to_row[:, s, j:j + 1], axis=0),
                                            in_=y_out[:, s, j, :], in_offset=None, bounds_check=TOKENS - 1,
                                            oob_is_err=False).then_inc(s_out[s], 16)

            def move(t):
                gather(Turn(t.group, t.step + UT, UT, NT), s_from[t.slot(UT)])
                scatter(t)

            for k in range(UT):
                gather(Turn(0, k, UT, NT), s_first)
            every_turn(pool, UT, NT, move, NTG - UT)
            for t in range(NTG - UT, NT):
                scatter(Turn(t // UT, t % UT, UT, NT))

        @block.scalar
        def _(act):
            def split_hi(k):
                act.wait_ge(s_wl[k % 2], 32 * (k // 2 + 1))
                if k >= 2:
                    act.wait_ge(s_ws[k % 2], 16 * (k // 2))
                for e in range(2):
                    last = act.activation(w_split[:, k % 2, e, 0], w_in[:, k % 2, e], ACT.Copy)
                last.then_inc(s_whi, 1)

            def gates(t):
                if t.real:
                    wait_turn(act, s_gate, 1, t, 1)
                    wait_turn(act, s_tout, 2, t, -2)
                    wait_turn(act, s_tloop, 1, t, -1)
                    for k in range(3):
                        bias = gate_b[:, k:k + 1] if k < 2 else 0.0
                        last = act.activation(sig[:, t.slot(2), k, :], ps_gate[:, :, k], ACT.Sigmoid, bias=bias)
                    last.then_inc(s_sig, 1)

            def times_in(t):
                if t.real:
                    wait_turn(act, s_sig, 1, t, 1)
                    wait_turn(act, s_tsum, 1, t, 0)
                    for k in range(2):
                        wait_turn(act, s_prod, 2, t, k + 1)
                        for b in range(4 * k, 4 * k + 4):
                            last = act.activation(t_in[:, b, :], ps_in[:, k, b % 4, :], ACT.Copy, scale=sig[:, t.slot(2), 0, b:b + 1])
                        last.then_inc(s_tin, 1)

            def norm1(t, turn_):
                if t.real:
                    wait_turn(act, s_norms, 1, turn_, 0)
                    wait_turn(act, s_prod, 2, t, -2)
                    wait_turn(act, s_tloop, 1, t, -1)
                    for b in range(G):
                        last = act.activation(hs[:, t.slot(2), b, :], xs[:, t.slot(4), b, :], ACT.Identity,
                                              scale=rstd[:, 0, b:b + 1], bias=shift[:, 0, b:b + 1])
                    last.then_inc(s_h, 1)

            def norm2(t, turn_):
                if t.real:
                    wait_turn(act, s_norms, 1, turn_, 0)
                    for b in range(G):
                        last = act.activation(row[:, t.slot(4), b, 0:P], row[:, t.slot(4), b, P:2 * P], ACT.Identity,
                                              scale=rstd[:, 1, b:b + 1], bias=shift[:, 1, b:b + 1])
                    last.then_inc(s_h2, 1)

            def copy_t(t, s_from, s_done_, dst, s_free):
                if t.real:
                    wait_turn(act, s_free, 1, t, 0)
                    for k in range(2):
                        wait_turn(act, s_from, 2, t, k + 1)
                        act.activation(dst[:, 4 * k:4 * k + 4, :], ps_t[:, k], ACT.Copy).then_inc(s_done_, 1)

            def row_weights(t):
                if t.real:
                    wait_turn(act, s_margin, 1, t, 1)
                    act.activation(row[:, t.slot(4), :, 2 * P], margin[:], ACT.Sigmoid)
                    act.activation(row[:, t.slot(4), :, 2 * P + 1], margin[:], ACT.Sigmoid, scale=-1.0).then_inc(s_rw, 1)

            def store_row(t):
                if t.real:
                    wait_turn(act, s_rw, 1, t, 1)
                    b = t.index * G
                    act.dma_start(rows_by_node[:, bass.ds(b, G), :], row[:, t.slot(4)]).then_inc(s_row[t.slot(4)], 16)

            def turn(t):
                if isinstance(t.index, int) and t.index < E // 2:
                    split_hi(2 * t.index)
                    split_hi(2 * t.index + 1)
                norm1(t.back(1), t)
                row_weights(t.back(6))
                norm2(t.back(4), t)
                store_row(t.back(6))
                times_in(t.back(2))
                copy_t(t.back(1), s_ht_ps, s_ht, hT, s_gate)
                copy_t(t.back(4), s_h2t_ps, s_h2t, h2T, s_logit)
                gates(t.back(1))

            act.wait_ge(s_small, 16 * 10)
            act.wait_ge(s_const, N_CONST)
            act.activation(ident_r[:], ident[:], ACT.Copy).then_inc(s_adj, 1)
            every_turn(act, UA, CHUNKS, turn, **GRAPH_LOOP)

            def times_node(t):
                wait_turn(act, s_hot, 1, t, 1)
                wait_turn(act, s_inv, 1, t, -1)
                act.activation(at_row_n[:, t.slot(2)], at_row[:, t.slot(2)], ACT.Copy, scale=node_f[:]).then_inc(s_hot_n, 1)

            act.wait_ge(s_iota, 6)
            for k in range(2):
                times_node(Turn(0, k, 2, CHUNKS))
            with act.Fori(1, CHUNKS // 2) as g:
                for k in range(2):
                    times_node(Turn(g, k, 2, CHUNKS))

            act.wait_ge(s_b_ps, 1)
            act.activation(b_of_tile[:], ps_bias, ACT.Copy).then_inc(s_btab, 1)

            def tile_hi(t):
                wait_turn(act, s_xt, 1, t, 1)
                wait_turn(act, s_mm1[1], 2, t, -2)
                act.activation(in_hi[:, t.slot(2)], ps_x, ACT.Copy).then_inc(s_inhi, 1)

            def gelu(t, s):
                wait_turn(act, s_split[s], 2, t, 0)
                if s == 0:
                    wait_slot(act, s_bt, 1, t, 1)
                for c in range(FC):
                    if c % 2 == 0:
                        wait_turn(act, s_mm1[s], 2, t, c // 2 + 1)
                    act.activation(act_f[:, s, c, :], ps_h[s][:, c, :], ACT.Gelu, bias=b_t[:, t.slot(UT), c, s:s + 1]).then_inc(s_act[s], 1)

            def copy_y(t, s):
                if t.real:
                    wait_turn(act, s_mm2[s], 1, t, 1)
                    wait_turn(act, s_o, 1, t, 0)
                    act.activation(y_t[:, s, :], ps_y[s], ACT.Identity, bias=b_t[:, t.slot(UT), FC, s:s + 1]).then_inc(s_y[s], 1)

            def tile(t):
                gelu(t, 0)
                copy_y(t.back(1), 1)
                tile_hi(Turn(t.group, t.step + 1, UT, NT))
                gelu(t, 1)
                copy_y(t, 0)

            tile_hi(Turn(0, 0, UT, NT))
            every_turn(act, UT, NT, tile)
            copy_y(END.back(1), 1)

        @block.vector
        def _(dve):
            own = Own(dve, s_dve)

            dve.wait_ge(s_const, N_CONST)
            dve.tensor_copy(iota_f[:], iota_i[:]).then_inc(s_iota, 1)
            dve.tensor_copy(iota_b[:], iota_i[:]).then_inc(s_iota, 1)
            dve.tensor_scalar(graph_b[:], iota_i[:, 0:NB], 1.0, None, ALU.add).then_inc(s_iota, 1)
            dve.tensor_copy(node_f[:], node_i[:]).then_inc(s_iota, 1)
            dve.tensor_scalar(node_b[:, 0:1], node_i[:], -1.0, None, ALU.add).then_inc(s_iota, 1)
            dve.tensor_scalar(node_b[:, 1:2], node_i[:], 0.0, None, ALU.is_equal).then_inc(s_iota, 1)

            dve.wait_ge(s_small, 16 * 10)
            dve.wait_ge(s_adjt, 1)
            own(dve.tensor_copy(adj_t[:], ps_t[:, 0, 0, :]))
            own(dve.scalar_tensor_tensor(out=tmp_m[:, 1, :], in0=adj_s[:], scalar=0.0, in1=adj_s[:], op0=ALU.is_le, op1=ALU.mult))
            own.sync()
            own(dve.scalar_tensor_tensor(out=tmp_m[:, 0, :], in0=adj_t[:], scalar=0.0, in1=adj_t[:], op0=ALU.is_le, op1=ALU.mult))
            own.sync()
            own(dve.scalar_tensor_tensor(out=adj_out[:], in0=adj_s[:], scalar=0.0, in1=tmp_m[:, 1, :], op0=ALU.is_gt, op1=ALU.add))
            own(dve.scalar_tensor_tensor(out=adj_in[:], in0=adj_t[:], scalar=0.0, in1=tmp_m[:, 0, :], op0=ALU.is_gt, op1=ALU.add))
            own.sync()
            own(dve.tensor_tensor(tmp_m[:, 0, :], adj_in[:], adj_t[:], ALU.mult))
            own(dve.tensor_tensor(tmp_m[:, 1, :], adj_out[:], adj_t[:], ALU.mult))
            own.sync()
            dve.tensor_copy(adj_in[:], tmp_m[:, 0, :]).then_inc(s_adj, 1)
            dve.tensor_copy(adj_out[:], tmp_m[:, 1, :]).then_inc(s_adj, 1)
            for k in range(2):
                src = eb[:, k, :].unsqueeze(1).to_broadcast([P, 4, P])
                own(dve.tensor_copy(eb_hi[:, k], src))
                own.sync()
                dve.tensor_tensor(eb_lo[:, k], src, eb_hi[:, k].bitcast(F32), ALU.subtract).then_inc(s_adj, 1)

            def turn(t):
                one, mid, two, rt_ = t, t.back(2), t.back(3), t.back(5)
                norms = one.real or two.real

                if one.real:
                    wait_slot(dve, s_x, 16, one, 16)
                    for b in range(G):
                        own(dve.bn_stats(stats[:, 0, b, :], xs[:, one.slot(4), b, :]))
                if two.real:
                    wait_turn(dve, s_tsum, 1, two, 1)
                    wait_slot(dve, s_row, 16, two, 0)
                    dve.scalar_tensor_tensor(out=row[:, two.slot(4), :, P:2 * P], in0=t_sum[:], scalar=0.0,
                                             in1=xs[:, two.slot(4)], op0=ALU.max, op1=ALU.add).then_inc(s_x1, 1)
                if rt_.real:
                    wait_turn(dve, s_logit, 1, rt_, 1)
                    dve.tensor_tensor(logit[:], ps_logit, bg_s[:].unsqueeze(1).to_broadcast([P, G, E]), ALU.add).then_inc(s_lsum, 1)
                if two.real:
                    wait_turn(dve, s_x1, 1, two, 1)
                    for b in range(G):
                        own(dve.bn_stats(stats[:, 1, b, :], row[:, two.slot(4), b, P:2 * P]))
                if mid.real:
                    wait_turn(dve, s_tloop, 1, mid, 1)
                    wait_turn(dve, s_x1, 1, mid, 0)

                def times_out(b):
                    if mid.real:
                        if b % 4 == 0:
                            wait_turn(dve, s_prod, 2, mid, b // 4 + 1)
                        ins = dve.scalar_tensor_tensor(out=t_sum[:, b, :], in0=ps_out[:, b // 4, b % 4, :],
                                                       scalar=sig[:, mid.slot(2), 1, b:b + 1], in1=t_loop[:, b, :],
                                                       op0=ALU.mult, op1=ALU.add)
                        if b % 4 == 3:
                            ins.then_inc(s_tout, 1)

                msum, mdiff, m2, dd, var, y, a, c = (ln_tmp[:, i] for i in range(8))
                low, high, order, sign, diff, half, prod, class_ = (rt[:, i, :] for i in range(8))
                if rt_.real:
                    b0 = rt_.index * G
                    wait_turn(dve, s_lsum, 1, rt_, 1)
                own.sync()
                if norms:
                    st = stats[:]
                    own(dve.tensor_tensor(msum, st[:, :, :, 1], st[:, :, :, 4], ALU.add))
                    own(dve.tensor_tensor(mdiff, st[:, :, :, 1], st[:, :, :, 4], ALU.subtract))
                    own(dve.tensor_tensor(m2, st[:, :, :, 2], st[:, :, :, 5], ALU.add))
                if rt_.real:
                    for b in range(G):
                        own(dve.max(top[:, b, :], logit[:, b, :]))
                own.sync()
                if norms:
                    own(dve.tensor_tensor(dd, mdiff, mdiff, ALU.mult))
                if rt_.real:
                    own(dve.tensor_tensor(diff, top[:, :, 0], top[:, :, 1], ALU.subtract))
                    for b in range(G):
                        own(dve.max_index(top_at[:, b, :], top[:, b, :], logit[:, b, :]))
                own.sync()
                if norms:
                    own(dve.scalar_tensor_tensor(out=a, in0=dd, scalar=D / 4.0, in1=m2, op0=ALU.mult, op1=ALU.add))
                if rt_.real:
                    i0, i1 = top_at[:, :, 0], top_at[:, :, 1]
                    own(dve.tensor_tensor(low, i0, i1, ALU.min))
                    own(dve.tensor_tensor(high, i0, i1, ALU.max))
                    own(dve.tensor_tensor(order, i0, i1, ALU.is_lt))
                own.sync()
                if norms:
                    own(dve.tensor_scalar(var, a, 1.0 / D, EPS, ALU.mult, ALU.add))
                if rt_.real:
                    own(dve.tensor_scalar(sign, order, 2.0, -1.0, ALU.mult, ALU.add))
                    own(dve.tensor_scalar(half, low, -0.5, E - 1.5, ALU.mult, ALU.add))
                times_out(0)
                own.sync()
                if norms:
                    own(dve.tensor_scalar(ln_bits[:, 0], var.bitcast(I32), 1, None, ALU.logical_shift_right))
                if rt_.real:
                    wait_turn(dve, s_rw, 1, rt_, 0)
                    dve.tensor_tensor(margin[:], diff, sign, ALU.mult).then_inc(s_margin, 1)
                    own(dve.tensor_tensor(prod, half, low, ALU.mult))
                own.sync()
                if norms:
                    own(dve.tensor_scalar(ln_bits[:, 1], ln_bits[:, 0], -1.0, RSQRT_SEED, ALU.mult, ALU.add))
                if rt_.real:
                    own(dve.scalar_tensor_tensor(out=class_, in0=prod, scalar=-1.0, in1=high, op0=ALU.add, op1=ALU.add))
                times_out(1)
                own.sync()
                now = ln_bits[:, 1].bitcast(F32)
                if norms:
                    own(dve.tensor_tensor(a, now, now, ALU.mult))
                if rt_.real:
                    own(dve.tensor_copy(class_of[:, bass.ds(b0, G)], class_))
                    own(dve.tensor_copy(hot[:, :, 0:1], count[:, :, G:G + 1]))
                    own(dve.tensor_tensor(hot[:, :, 1:G + 1], iota_f[:, 0:NCLASS].unsqueeze(2).to_broadcast([P, NCLASS, G]),
                                          class_.unsqueeze(1).to_broadcast([P, NCLASS, G]), ALU.is_equal))
                own.sync()
                if norms:
                    own(dve.scalar_tensor_tensor(out=c, in0=a, scalar=-0.5, in1=var, op0=ALU.mult, op1=ALU.mult))
                if rt_.real:
                    own(dve.tensor_tensor_scan(count[:].rearrange("p c g -> p (c g)"), keep[:].rearrange("p c g -> p (c g)"),
                                               hot[:].rearrange("p c g -> p (c g)"), 0.0, ALU.mult, ALU.add))
                own.sync()
                if norms:
                    own(dve.scalar_tensor_tensor(out=y, in0=c, scalar=1.5, in1=now, op0=ALU.add, op1=ALU.mult))
                if rt_.real:
                    own(dve.tensor_tensor(ranked[:], hot[:, :, 1:G + 1], count[:, :, 0:G], ALU.mult))
                own.sync()
                if norms:
                    own(dve.tensor_tensor(a, y, y, ALU.mult))
                if rt_.real:
                    own(dve.tensor_reduce(rank_of[:, bass.ds(b0, G)], ranked[:].rearrange("p c g -> p g c"), AX_X, ALU.add))
                times_out(2)
                own.sync()
                if norms:
                    own(dve.scalar_tensor_tensor(out=c, in0=a, scalar=-0.5, in1=var, op0=ALU.mult, op1=ALU.mult))
                times_out(3)
                own.sync()
                if norms:
                    own(dve.scalar_tensor_tensor(out=dd, in0=c, scalar=1.5, in1=y, op0=ALU.add, op1=ALU.mult))
                times_out(4)
                own.sync()
                if norms:
                    own(dve.tensor_tensor(a, dd, dd, ALU.mult))
                times_out(5)
                own.sync()
                if norms:
                    own(dve.scalar_tensor_tensor(out=c, in0=a, scalar=-0.5, in1=var, op0=ALU.mult, op1=ALU.mult))
                times_out(6)
                own.sync()
                if norms:
                    if one.real:
                        wait_turn(dve, s_h, 1, one, 0)
                    else:
                        dve.wait_ge(s_h, CHUNKS)
                    wait_turn(dve, s_h2, 1, two, 0)
                    own(dve.scalar_tensor_tensor(out=rstd[:], in0=c, scalar=1.5, in1=dd, op0=ALU.add, op1=ALU.mult))
                times_out(7)
                own.sync()
                if norms:
                    dve.scalar_tensor_tensor(out=shift[:], in0=msum, scalar=-0.5, in1=rstd[:],
                                             op0=ALU.mult, op1=ALU.mult).then_inc(s_norms, 1)

            own(dve.memset(count[:], 0.0))
            own(dve.memset(stats[:], 1.0))
            own.sync()
            every_turn(dve, UA, CHUNKS, turn, own=own, **GRAPH_LOOP)

            own.sync()
            dve.tensor_copy(totals[:], count[:, :, G]).then_inc(s_tot, 1)
            dve.wait_ge(s_tot_ps, 1)
            tiles_f, upto, base, offset, ones_c = (pl[:, i, :] for i in range(5))
            own(dve.tensor_scalar(pl_i[:, 0, :], ps_tot, TILE - 1.0, None, ALU.add))
            own(dve.memset(ones_c, 1.0))
            own.sync()
            own(dve.tensor_scalar(pl_i[:, 1, :], pl_i[:, 0, :], TILE.bit_length() - 1, None, ALU.logical_shift_right))
            own.sync()
            own(dve.tensor_copy(tiles_f, pl_i[:, 1, :]))
            own.sync()
            own(dve.tensor_tensor_scan(upto, ones_c, tiles_f, 0.0, ALU.mult, ALU.add))
            own.sync()
            own(dve.tensor_tensor(base, upto, tiles_f, ALU.subtract))
            own.sync()
            own(dve.scalar_tensor_tensor(out=offset, in0=base, scalar=float(TILE), in1=ps_pre, op0=ALU.mult, op1=ALU.add))
            own(dve.tensor_scalar(started[:, 0, :], base, node_f[:], None, ALU.is_le))
            own(dve.tensor_scalar(started[:, 1, :], base, node_b[:, 0:1], None, ALU.is_le))
            own.sync()
            for k in range(2):
                for s in range(2):
                    own(dve.tensor_tensor(steps[:, 2 * k + s, :], started[:, k, :], step_e[:, s, :], ALU.mult))
            own.sync()
            own(dve.tensor_reduce(expert[:], steps[:], AX_X, ALU.add))
            own.sync()
            dve.tensor_copy(expert_rep[:], expert[:, 0:2].unsqueeze(2).to_broadcast([P, 2, E])).then_inc(s_rep, 1)
            own(dve.tensor_tensor(change[:, 0, :], expert[:, 0:2], expert[:, 2:4], ALU.subtract))
            own.sync()
            own(dve.tensor_tensor(change[:, 1, :], change[:, 0, :], change[:, 0, :], ALU.mult))
            own.sync()
            own(dve.tensor_scalar(change[:, 2, :], change[:, 1, :], node_b[:, 1:2], 0.0, ALU.add, ALU.is_gt))
            own.sync()
            own(dve.scalar_tensor_tensor(out=change[:, 0, :], in0=expert[:, 0:2], scalar=-float(E), in1=change[:, 2, :], op0=ALU.add, op1=ALU.mult))
            own.sync()
            own(dve.tensor_scalar(change[:, 1, :], change[:, 0, :], float(E), None, ALU.add))
            own.sync()
            dve.scalar_tensor_tensor(out=code[:], in0=change[:, 1, 0:1], scalar=16.0, in1=change[:, 1, 1:2],
                                     op0=ALU.mult, op1=ALU.add).then_inc(s_texp, 1)
            dve.wait_ge(s_exp_ps, 1)
            dve.tensor_scalar(expert_hot[:], ps_exp, node_f[0:E, :], None, ALU.is_equal).then_inc(s_exp_hot, 1)

            def one_hots(t, b0):
                s = t.slot(2)
                own(dve.tensor_tensor(pick[:, 0], iota_f[:, 0:NCLASS].unsqueeze(1).to_broadcast([P, G, NCLASS]),
                                      class_of[:, bass.ds(b0, G)].unsqueeze(2).to_broadcast([P, G, NCLASS]), ALU.is_equal))
                own.sync()
                own(dve.tensor_tensor(pick[:, 1], pick[:, 0], offset.unsqueeze(1).to_broadcast([P, G, NCLASS]), ALU.mult))
                own.sync()
                own(dve.tensor_reduce(place[:, s, :], pick[:, 1], AX_X, ALU.add))
                own.sync()
                own(dve.tensor_tensor(place_i[:, 0, s, :], place[:, s, :], rank_of[:, bass.ds(b0, G)], ALU.add))
                own.sync()
                own(dve.tensor_scalar(place_i[:, 1, s, :], place_i[:, 0, s, :], P - 1, None, ALU.bitwise_and))
                own(dve.tensor_scalar(place_i[:, 2, s, :], place_i[:, 0, s, :], P.bit_length() - 1, None, ALU.logical_shift_right))
                own.sync()
                wait_turn(dve, s_inv, 1, t, -1)
                wait_turn(dve, s_hot_n, 1, t, -1)
                wait_turn(dve, s_hot_b, 1, t, -1)
                dve.tensor_tensor(at_row[:, s], iota_b[:, 0:P].unsqueeze(1).to_broadcast([P, G, P]),
                                  place_i[:, 1, s, :].unsqueeze(2).to_broadcast([P, G, P]), ALU.is_equal).then_inc(s_hot, 1)
                dve.tensor_tensor(at_col[:, s], iota_b[:, 0:COLS].unsqueeze(1).to_broadcast([P, G, COLS]),
                                  place_i[:, 2, s, :].unsqueeze(2).to_broadcast([P, G, COLS]), ALU.is_equal).then_inc(s_hot_c, 1)

            for k in range(2):
                n0 = own.n
                one_hots(Turn(0, k, 2, CHUNKS), k * G)
                own_each = own.n - n0
            with dve.Fori(1, CHUNKS // 2) as g:
                own.enter(g, 1, 2 * own_each)
                for k in range(2):
                    t = Turn(g, k, 2, CHUNKS)
                    one_hots(t, t.index * G)
                own.leave(CHUNKS // 2 - 1)

            dve.wait_ge(s_inv, CHUNKS + 1)
            node, graph, empty, target = (inv[:, i, :] for i in range(4))
            own(dve.tensor_copy(node, ps_a))
            own(dve.tensor_copy(graph, ps_b))
            own.sync()
            shaped = lambda a: a.rearrange("p (t j) -> p t j", j=BLK)
            own(dve.scalar_tensor_tensor(out=index[:, :, 0:BLK], in0=shaped(node), scalar=float(NB), in1=shaped(graph), op0=ALU.mult, op1=ALU.add))
            own(dve.tensor_scalar(empty, graph, 0.0, 4.0 * TOKENS, ALU.is_equal, ALU.mult))
            own(dve.scalar_tensor_tensor(out=target, in0=graph, scalar=float(N), in1=node, op0=ALU.mult, op1=ALU.add))
            own.sync()
            dve.scalar_tensor_tensor(out=index[:, :, BLK:2 * BLK], in0=shaped(target), scalar=-float(N), in1=shaped(empty),
                                     op0=ALU.add, op1=ALU.add).then_inc(s_index, 1)

            def tile_lo(t):
                wait_turn(dve, s_inhi, 1, t, 1)
                k = t.slot(2)
                dve.tensor_tensor(in_lo[:, k], ps_x, in_hi[:, k].bitcast(F32), ALU.subtract).then_inc(s_inlo, 1)

            def split(t, s):
                wait_turn(dve, s_mm2[s], 1, t, 0)
                for k in range(2):
                    cs = slice(k * FC // 2, (k + 1) * FC // 2)
                    wait_turn(dve, s_act[s], FC, t, (k + 1) * FC // 2)
                    dve.tensor_copy(act_hi[:, s, cs, :], act_f[:, s, cs, :]).then_inc(s_hhi, 1)
                    wait_turn(dve, s_hhi, 4, t, 2 * s + k + 1)
                    dve.tensor_tensor(act_lo[:, s, cs, :], act_f[:, s, cs, :], act_hi[:, s, cs, :].bitcast(F32),
                                      ALU.subtract).then_inc(s_split[s], 1)

            def sum_up(t):
                if t.real:
                    i = t.slot(UT)
                    wait_turn(dve, s_o, 1, t, 1)
                    for j in range(BLK):
                        last = dve.scalar_tensor_tensor(out=y_one[:, j, :], in0=ps_o[:, 0, j, :], scalar=got[:, i, j, 2 * P:2 * P + 1],
                                                        in1=got[:, i, j, P:2 * P], op0=ALU.mult, op1=ALU.add)
                    last.then_inc(s_y1, 1)
                    wait_turn(dve, s_y1, 1, t, 1)
                    wait_slot(dve, s_out, 16 * BLK, t, 0)
                    for j in range(BLK):
                        last = dve.scalar_tensor_tensor(out=y_out[:, i, j, :], in0=ps_o[:, 1, j, :], scalar=got[:, i, j, 2 * P + 1:2 * P + 2],
                                                        in1=y_one[:, j, :], op0=ALU.mult, op1=ALU.add)
                    last.then_inc(s_done[i], 1)

            def tile(t):
                split(t, 0)
                tile_lo(Turn(t.group, t.step + 1, UT, NT))
                split(t, 1)
                sum_up(t.back(1))

            tile_lo(Turn(0, 0, UT, NT))
            every_turn(dve, UT, NT, tile)
            sum_up(END.back(1))

        @block.tensor
        def _(pe):
            pe.wait_ge(s_const, N_CONST)
            pe.wait_ge(s_small, 16 * 10)
            pe.transpose(ps_t[:, 0, 0, :], adj_s[:], ident[:]).then_inc(s_adjt, 1)
            pe.wait_ge(s_adj, 5)

            def transposed(t, src, s_src, s_dst, bank_free, more):
                wait_turn(pe, s_src, 1, t, 1)
                for b in range(G):
                    if b % 4 == 0:
                        wait_turn(pe, *bank_free, more + b // 4)
                    last = pe.transpose(ps_t[:, b // 4, b % 4, :], src(b), ident[:])
                    if b % 4 == 3:
                        last.then_inc(s_dst, 1)

            def products(t):
                if t.real:
                    wait_turn(pe, s_h, 1, t, 1)
                    for k in range(2):
                        rhs = hs[:, t.slot(2), 4 * k:4 * k + 4, :]
                        wait_turn(pe, s_tin, 2, t, k - 1)
                        wait_turn(pe, s_tout, 2, t, k - 1)
                        for dst, w, e in ((ps_in, adj_in, 0), (ps_out, adj_out, 1)):
                            pe.matmul(dst[:, k], w[:], rhs, start=True, stop=False)
                            pe.matmul(dst[:, k], ident_r[:], eb_hi[:, e], start=False, stop=False)
                            last = pe.matmul(dst[:, k], ident_r[:], eb_lo[:, e], start=False, stop=True)
                        last.then_inc(s_prod, 1)

            def small(t, s_src, src, w, dst, s_free, s_dst):
                if t.real:
                    wait_turn(pe, s_src, 2, t, 2)
                    wait_turn(pe, s_free, 1, t, 0)
                    for b in range(G):
                        last = pe.matmul(dst(b), src[:, b, :], w[:], start=True, stop=True)
                    last.then_inc(s_dst, 1)

            def turn(t):
                one, two = t.back(1), t.back(4)
                products(t.back(2))
                h2t_before = (s_h2t, 2, two)
                if one.real:
                    transposed(one, lambda b: hs[:, one.slot(2), b, :], s_h, s_ht_ps, h2t_before, -1)
                if two.real:
                    transposed(two, lambda b: row[:, two.slot(4), b, 0:P], s_h2, s_h2t_ps,
                               *(((s_ht, 2, one), 1) if one.real else (h2t_before, -1)))
                small(one, s_ht, hT, gate_w, lambda b: ps_gate[:, b, 0:3], s_sig, s_gate)
                small(two, s_h2t, h2T, wg_s, lambda b: ps_logit[:, b, :], s_lsum, s_logit)

            every_turn(pe, UA, CHUNKS, turn, **GRAPH_LOOP)

            pe.wait_ge(s_tot, 1)
            pe.matmul(ps_pre, before[:], totals[:], start=True, stop=True)
            pe.matmul(ps_tot, ones_b[:], totals[:], start=True, stop=True).then_inc(s_tot_ps, 1)

            pe.wait_ge(s_rep, 1)
            pe.wait_ge(s_bias, 32)
            for s in range(2):
                last = pe.matmul(ps_exp[:, s, :], expert_rep[:, s, :], ident[:], start=True, stop=True)
            last.then_inc(s_exp_ps, 1)
            pe.wait_ge(s_exp_hot, 1)
            for c in range(FC):
                pe.matmul(ps_bias[:, c], b1_s[:, c * P:(c + 1) * P], expert_hot[:], start=True, stop=True)
            last = pe.matmul(ps_bias[:, FC], b2_s[:], expert_hot[:], start=True, stop=True)
            last.then_inc(s_b_ps, 1)

            def inverse(t):
                wait_turn(pe, s_hot_n, 1, t, 1)
                wait_turn(pe, s_hot_b, 1, t, 1)
                s = t.slot(2)
                wait_turn(pe, s_hot_c, 1, t, 1)
                for b in range(G):
                    pe.matmul(ps_a, at_row_n[:, s, b, :], at_col[:, s, b, :], start=False, stop=False)
                    last = pe.matmul(ps_b, at_row_b[:, s, b, :], at_col[:, s, b, :], start=False, stop=False)
                last.then_inc(s_inv, 1)

            for dst in (ps_a, ps_b):
                pe.matmul(dst, zeros_b[:, 0:P], zeros_b[:], start=True, stop=False)
            for k in range(2):
                inverse(Turn(0, k, 2, CHUNKS))
            with pe.Fori(1, CHUNKS // 2) as g:
                for k in range(2):
                    inverse(Turn(g, k, 2, CHUNKS))
            for dst in (ps_a, ps_b):
                last = pe.matmul(dst, zeros_b[:, 0:P], zeros_b[:], start=False, stop=True)
            last.then_inc(s_inv, 1)

            pe.wait_ge(s_btab, 1)

            def tile_in(t):
                s = t.slot(UT)
                wait_slot(pe, s_got, 16 * BLK, t, 16 * BLK)
                wait_turn(pe, s_inlo, 1, t, 0)
                for j in range(BLK):
                    last = pe.transpose(ps_x[:, j * P:(j + 1) * P], got[:, s, j, 0:P], ident[:])
                last.then_inc(s_xt, 1)

            def layer1(t, s):
                k = t.slot(2)
                wait_turn(pe, s_wt[0][s], 16, t, 16)
                wait_turn(pe, s_inlo, 1, t, 1)
                wait_turn(pe, s_inhi, 1, t, 1)
                wait_turn(pe, s_act[s], FC, t, 0)
                for c in range(FC):
                    hi = wt[0][:, s, c * P:(c + 1) * P]
                    lo = wt[0][:, s, H + c * P:H + (c + 1) * P]
                    pe.matmul(ps_h[s][:, c, :], hi, in_hi[:, k], start=True, stop=False)
                    pe.matmul(ps_h[s][:, c, :], hi, in_lo[:, k], start=False, stop=False)
                    last = pe.matmul(ps_h[s][:, c, :], lo, in_hi[:, k], start=False, stop=True)
                    if c % 2:
                        last.then_inc(s_mm1[s], 1)

            def layer2(t, s):
                if t.real:
                    wait_turn(pe, s_wt[1][s], 16, t, 16)
                    wait_turn(pe, s_y[s], 1, t, 0)
                    for c in range(FC):
                        if c % 2 == 0:
                            wait_turn(pe, s_split[s], 2, t, c // 2 + 1)
                        hi = wt[1][:, s, c * P:(c + 1) * P]
                        lo = wt[1][:, s, H + c * P:H + (c + 1) * P]
                        pe.matmul(ps_y[s], hi, act_hi[:, s, c, :], start=(c == 0), stop=False)
                        pe.matmul(ps_y[s], hi, act_lo[:, s, c, :], start=False, stop=False)
                        last = pe.matmul(ps_y[s], lo, act_hi[:, s, c, :], start=False, stop=(c == FC - 1))
                    last.then_inc(s_mm2[s], 1)

            def tile_out(t):
                if t.real:
                    for s in range(2):
                        wait_turn(pe, s_y[s], 1, t, 1)
                    wait_slot(pe, s_done, 1, t.back(1), 1)
                    for s in range(2):
                        for j in range(BLK):
                            last = pe.transpose(ps_o[:, s, j, :], y_t[:, s, j * P:(j + 1) * P], ident[:])
                    last.then_inc(s_o, 1)

            def tile(t):
                layer1(t, 0)
                layer2(t.back(1), 1)
                tile_in(Turn(t.group, t.step + 1, UT, NT))
                layer1(t, 1)
                tile_out(t.back(1))
                layer2(t, 0)

            tile_in(Turn(0, 0, UT, NT))
            every_turn(pe, UT, NT, tile)
            layer2(END.back(1), 1)
            tile_out(END.back(1))


_INS = ["x", "adj", "L0_gnn_edge_bias", "L0_gnn_gate_weight", "L0_gnn_bias_gate", "L0_gnn_out_edge_bias",
        "L0_gnn_out_gate_weight", "L0_gnn_out_bias_gate", "L0_gnn_loop_gate", "L0_ffn_Wg", "L0_ffn_bg",
        "L0_ffn_W1", "L0_ffn_b1", "L0_ffn_W2", "L0_ffn_b2"]


def kernel(**inputs):
    import numpy as _np
    import concourse.bacc as _bacc
    from concourse import mybir as _mybir
    from concourse.bass_utils import run_bass_kernel_spmd as _run

    nc = _bacc.Bacc("TRN2", target_bir_lowering=False, num_devices=1)
    arrays, args = {}, []
    for name in _INS:
        a = _np.ascontiguousarray(inputs[name])
        arrays[f"in_{name}_dram"] = a
        args.append(nc.dram_tensor(f"in_{name}_dram", a.shape, _mybir.dt.from_np(a.dtype), kind="ExternalInput").ap())
    shape = inputs["x"].shape
    args.append(nc.dram_tensor("out_0_dram", shape, _mybir.dt.float32, kind="ExternalOutput").ap())
    program(nc, *args)
    r = _run(nc, [arrays], core_ids=[0])
    return r.results[0]["out_0_dram"]
```

```python
from contextlib import ExitStack

import concourse.bass as bass
from concourse import mybir

F32 = mybir.dt.float32
F32R = mybir.dt.float32r
BF16 = mybir.dt.bfloat16
I32 = mybir.dt.int32
U32 = mybir.dt.uint32
ALU = mybir.AluOpType
ACT = mybir.ActivationFunctionType
AX_X = mybir.AxisListType.X

P = 128
G = 8
E = 8
EPS = 1e-5
RSQRT_SEED = float(0x5F3759DF)
FIRST = [(a, b) for a in range(E) for b in range(a + 1, E)]
NCLASS = len(FIRST)
TILE = 256
BLK = TILE // P
ROW = 2 * P + 4


class Turn:

    def __init__(self, group, step, unroll, total):
        self.group, self.step, self.unroll, self.total = group, step, unroll, total
        self.index = group * unroll + step

    def back(self, n):
        return Turn(self.group, self.step - n, self.unroll, self.total)

    def slot(self, ring):
        assert self.unroll % ring == 0
        return self.step % ring

    @property
    def real(self):
        return not isinstance(self.index, int) or 0 <= self.index < self.total


def wait_turn(eng, sem, each, turn, more):
    value = turn.group * (each * turn.unroll) + (each * turn.step + more)
    if not isinstance(value, int) or value > 0:
        eng.wait_ge(sem, value)


def wait_slot(eng, sems, each, turn, more):
    ring = len(sems)
    s = turn.slot(ring)
    wait_turn(eng, sems[s], each, Turn(turn.group, (turn.step - s) // ring, turn.unroll // ring, 0), more)


def apart(eng, sem):
    eng.wait_ge(sem, 1)


def every_turn(eng, unroll, total, body, until=None, first=1, own=None, last=None):
    until = total if until is None else until
    last = until // unroll if last is None else last
    for k in range(first * unroll):
        before = own.n if own else 0
        body(Turn(k // unroll, k % unroll, unroll, total))
        each = own.n - before if own else 0
    with eng.Fori(first, last) as g:
        if own:
            own.enter(g, first, unroll * each)
        for k in range(unroll):
            body(Turn(g, k, unroll, total))
        if own:
            own.leave(last - first)
    for k in range(last * unroll, until):
        body(Turn(k // unroll, k % unroll, unroll, total))


class Own:

    def __init__(self, eng, sem):
        self.eng, self.sem, self.base, self.n = eng, sem, 0, 0

    def __call__(self, ins):
        ins.then_inc(self.sem, 1)
        self.n += 1

    def sync(self):
        self.eng.wait_ge(self.sem, self.base + self.n)

    def enter(self, group, first, each):
        self.start, self.each = self.n, each
        self.base = (group * each) + (self.n - first * each)
        self.n = 0

    def leave(self, rounds):
        assert self.n == self.each, (self.n, self.each)
        self.base, self.n = 0, self.start + rounds * self.each


def program(nc, x, adj, edge_bias, gate_weight, bias_gate, out_edge_bias, out_gate_weight,
            out_bias_gate, loop_gate, Wg, bg, W1, b1, W2, b2, out):
    NB, N, D = x.shape
    H = W1.shape[2]
    assert N == P and D == P and NB % (4 * G) == 0 and W1.shape[0] == E
    FC = H // P
    CHUNKS = NB // G
    TOKENS = NB * N
    NT = TOKENS // TILE + NCLASS - 1
    NTG = NT + 1
    COLS = NTG * BLK
    HOTS = 4
    PIECE = HOTS * G
    BY_ACT = 6
    UA, UT = 4, 4
    END = Turn(NT // UT, NT % UT, UT, NT)
    assert CHUNKS % UA == 0
    GRAPH_LOOP = dict(until=CHUNKS + 6, first=2, last=CHUNKS // UA)

    def weight_steps(t):
        if not isinstance(t.index, int) or not 1 <= t.index < E:
            return []
        return [t.index - 1] if t.index < E - 1 else [E - 2, E - 1]


    w_dram = [nc.dram_tensor(f"w{l}_split", (16, P, 2 * H), F32).ap() for l in (1, 2)]
    rows = nc.dram_tensor("rows", (TOKENS + 1, ROW), F32).ap()
    rows_by_node = rows[1:TOKENS + 1, :].rearrange("(n b) k -> n b k", n=N)
    experts_dram = nc.dram_tensor("tile_experts", (NTG, 1), I32).ap()
    x_by_node = x.rearrange("b n d -> n b d")
    out_rows = out.rearrange("b n d -> (b n) d")

    with ExitStack() as ctx:
        def sb(name, shape, dt=F32):
            return ctx.enter_context(nc.sbuf_tensor(name, list(shape), dt))

        def sem(name):
            return ctx.enter_context(nc.semaphore(name))

        bank = ctx.enter_context(nc.psum_tensor("bank", [P, 8, 512], F32))

        ident = sb("ident", [P, P])
        ident_r = sb("ident_r", [P, P], F32R)
        ones_f = sb("ones_f", [P, P])
        before = sb("before", [P, P], BF16)
        ones_b = sb("ones_b", [P, P], BF16)
        zeros_b = sb("zeros_b", [P, COLS], BF16)
        iota_i = sb("iota_i", [P, 256], I32)
        iota_f = sb("iota_f", [P, 256])
        iota_b = sb("iota_b", [P, 256], BF16)
        graph_f = sb("graph_f", [P, NB])
        node_i = sb("node_i", [P, 1], I32)
        node_f = sb("node_f", [P, 1])
        step_e = sb("step_e", [P, 2, NCLASS])
        keep = sb("keep", [P, NCLASS, G + 1])
        adj_s = sb("adj_s", [P, P])
        adj_t = sb("adj_t", [P, P])
        tmp_m = sb("tmp_m", [P, 2, P])
        adj_in = sb("adj_in", [P, P])
        adj_out = sb("adj_out", [P, P])
        eb = sb("eb", [P, 2, P])
        eb_hi = sb("eb_hi", [P, 2, 4, P], F32R)
        eb_lo = sb("eb_lo", [P, 2, 4, P], F32R)
        gate_w = sb("gate_w", [P, 3])
        gate_b = sb("gate_b", [P, 2])
        wg_s = sb("wg_s", [P, E])
        bg_s = sb("bg_s", [P, E])
        xs = sb("xs", [P, 4, G, D])
        hs = sb("hs", [P, 2, G, D])
        row = sb("row", [P, 4, G, ROW])
        h_turned = sb("h_turned", [P, 2, G, P])
        hT, h2T = (h_turned[:, i] for i in range(2))
        t_three = sb("t_three", [P, 3, G, D])
        t_in, t_loop, t_sum = (t_three[:, i] for i in range(3))
        sig = sb("sig", [P, 2, 3, G])
        stats = sb("stats", [P, 2, G, 6])
        ln_tmp = sb("ln_tmp", [P, 8, 2, G])
        ln_bits = sb("ln_bits", [P, 2, 2, G], I32)
        rstd = sb("rstd", [P, 2, G])
        shift = sb("shift", [P, 2, G])
        logit = sb("logit", [P, G, E])
        top = sb("top", [P, G, 8])
        top_at = sb("top_at", [P, G, 8], U32)
        rt = sb("rt", [P, 8, G])
        margin = sb("margin", [P, G])
        hot = sb("hot", [P, NCLASS, G + 1])
        count = sb("count", [P, NCLASS, G + 1])
        ranked = sb("ranked", [P, NCLASS, G])
        class_of = sb("class_of", [P, NB])
        rank_of = sb("rank_of", [P, NB])
        totals = sb("totals", [P, NCLASS], BF16)
        pl = sb("pl", [P, 6, NCLASS])
        pl_i = sb("pl_i", [P, 2, NCLASS], I32)
        pick = sb("pick", [P, 2, PIECE, NCLASS])
        place = sb("place", [P, PIECE])
        place_i = sb("place_i", [P, PIECE], I32)
        place_at = sb("place_at", [P, PIECE], I32)
        row_at = sb("row_at", [P, NB], BF16)
        col_at = sb("col_at", [P, NB], I32)
        row_diff = sb("row_diff", [P, HOTS, G, P], BF16)
        def over(buffer, m):
            return buffer.rearrange("p a g d -> p (a g d)")[:, 0:HOTS * G * m // 2].bitcast(BF16).rearrange("p (r g m) -> p r g m", g=G, m=m)

        at_col, at_row = over(xs[:], COLS), over(h_turned[:], P)
        at_row_n, at_row_b = over(hs[:], P), over(t_three[:], P)
        inv = sb("inv", [P, 4, COLS])
        index = sb("index", [P, NTG, 2 * BLK], I32)
        started = sb("started", [P, 2, NCLASS])
        steps = sb("steps", [P, 4, NCLASS])
        node_b = sb("node_b", [P, 2])
        expert = sb("expert", [P, 4])
        change = sb("change", [P, 3, 2])
        code = sb("code", [P, 1], I32)
        expert_rep = sb("expert_rep", [P, 2, E])
        expert_hot = sb("expert_hot", [E, 2, P])
        b_of_tile = sb("b_of_tile", [P, FC + 1, 2, P])
        zero_row = sb("zero_row", [1, ROW])
        w_in = sb("w_in", [P, 2, 2, H])
        w_split = sb("w_split", [P, 2, 2, 2, H], F32R)
        b1_s = sb("b1_s", [E, H])
        b2_s = sb("b2_s", [E, D])
        wt = [sb(f"wt{l}", [P, 2, 2 * H], F32R) for l in (1, 2)]
        b_t = sb("b_t", [P, UT, FC + 1, 2])
        from_row = sb("from_row", [P, UT, BLK], I32)
        to_row = sb("to_row", [P, UT, BLK], I32)
        got = sb("got", [P, UT, BLK, ROW])
        in_hi = sb("in_hi", [P, 2, TILE], F32R)
        in_lo = sb("in_lo", [P, 2, TILE], F32R)
        act_f = w_in[:].rearrange("p s a (b m) -> p s (a b) m", m=TILE)
        act_hi, act_lo = (w_split[:, i].rearrange("p s a (b m) -> p s (a b) m", m=TILE) for i in range(2))
        y_t = sb("y_t", [P, 2, TILE])
        y_one = sb("y_one", [P, BLK, D])
        y_out = sb("y_out", [P, UT, BLK, D])

        ps_t = bank[:, 0:2, :].rearrange("p k (g m) -> p k g m", g=4)
        ps_in = bank[:, 2:4, :].rearrange("p k (g m) -> p k g m", g=4)
        ps_out = bank[:, 4:6, :].rearrange("p k (g m) -> p k g m", g=4)
        ps_gate = bank[:, 6, 0:4 * G].rearrange("p (g k) -> p g k", k=4)
        ps_logit = bank[:, 7, 64:64 + G * E].rearrange("p (g e) -> p g e", e=E)
        ps_pre = bank[:, 7, 0:NCLASS]
        ps_tot = bank[:, 7, 64:64 + NCLASS]
        ps_a = bank[:, 0, 0:COLS]
        ps_b = bank[:, 1, 0:COLS]
        ps_h = [bank[:, 2 * s:2 * s + 2, :].rearrange("p k (c m) -> p (k c) m", m=TILE) for s in range(2)]
        ps_y = [bank[:, 4 + s, 0:TILE] for s in range(2)]
        ps_x = bank[:, 6, 0:TILE]
        ps_o = bank[:, 7, :].rearrange("p (s j m) -> p s j m", s=2, j=BLK)
        ps_exp = bank[0:E, 2, 0:2 * P].rearrange("p (s t) -> p s t", s=2)
        ps_bias = bank[:, 4:7, :].rearrange("p k (c s t) -> p (k c) s t", s=2, t=P)[:, 0:FC + 1]

        s_const = sem("pool_constants")
        s_iota = sem("iota_copies")
        s_small = sem("small_inputs_loaded")
        s_bias = sem("biases_loaded")
        s_adjt = sem("adj_transposed")
        s_adj = sem("adj_matrices_ready")
        s_x = [sem(f"x_loaded{i}") for i in range(4)]
        s_norms = sem("norms_ready")
        s_h = sem("h_ready")
        s_ht_ps = sem("hT_in_psum")
        s_ht = sem("hT_copied")
        s_gate = sem("gates_in_psum")
        s_prod = sem("products_in_psum")
        s_sig = sem("sigmoids_ready")
        s_tloop = sem("t_loop_ready")
        s_tin = sem("t_in_ready")
        s_tout = sem("t_out_added")
        s_tsum = sem("t_sum_ready")
        s_x1 = sem("x1_ready")
        s_h2 = sem("h2_of_first_graphs_ready")
        s_h2b = sem("h2_of_last_graphs_ready")
        s_h2t_ps = sem("h2T_in_psum")
        s_h2t = sem("h2T_copied")
        s_logit = sem("logits_in_psum")
        s_lsum = sem("logits_read")
        s_margin = sem("margins_ready")
        s_rw = sem("row_weights_ready")
        s_row = [sem(f"row_stored{i}") for i in range(4)]
        s_dve = sem("dve_own")
        s_pool = sem("pool_own")
        s_tot = sem("totals_ready")
        s_tot_ps = sem("totals_in_psum")
        s_place = sem("places_of_piece_ready")
        s_diff = sem("row_differences_ready")
        s_hot = sem("row_hots_ready")
        s_hot_c = sem("column_hots_ready")
        s_hot_n = sem("row_hots_times_node")
        s_hot_b = sem("row_hots_times_graph")
        s_inv = sem("inverse_products")
        s_index = sem("index_ready")
        s_texp = sem("tile_experts_ready")
        s_tab = sem("tile_experts_stored")
        s_wl = [sem(f"w_staged{i}") for i in range(2)]
        s_whi = sem("w_hi_ready")
        s_wlo = sem("w_lo_ready")
        s_ws = [sem(f"w_split_stored{i}") for i in range(2)]
        s_bs = sem("zero_row_stored")
        s_rep = sem("tile_experts_repeated")
        s_exp_ps = sem("tile_experts_on_all_partitions")
        s_exp_hot = sem("tile_experts_one_hot")
        s_b_ps = sem("b_of_tiles_in_psum")
        s_btab = sem("b_of_tiles_copied")
        s_wt = [[sem(f"w{l}_of_slot{s}") for s in range(2)] for l in (1, 2)]
        s_first = sem("first_gather_indices_copied")
        s_from = [sem(f"gather_index_copied{i}") for i in range(UT)]
        s_to = [sem(f"scatter_index_copied{i}") for i in range(UT)]
        s_got = [sem(f"rows_gathered{i}") for i in range(UT)]
        s_xt = sem("tile_transposed")
        s_inhi = sem("tile_hi")
        s_inlo = sem("tile_lo")
        s_mm1 = [sem(f"hidden_in_psum{s}") for s in range(2)]
        s_act = [sem(f"gelu_done{s}") for s in range(2)]
        s_hhi = sem("hidden_hi")
        s_split = [sem(f"hidden_split{s}") for s in range(2)]
        s_mm2 = [sem(f"expert_out_in_psum{s}") for s in range(2)]
        s_y = [sem(f"expert_out_copied{s}") for s in range(2)]
        s_o = sem("outputs_transposed")
        s_bt = [sem(f"tile_b1_copied{i}") for i in range(UT)]
        s_y1 = sem("first_expert_added")
        s_done = [sem(f"tile_summed{i}") for i in range(UT)]
        s_out = [sem(f"rows_scattered{i}") for i in range(UT)]
        N_CONST = 14

        block = ctx.enter_context(nc.Block())

        @block.sync
        def _(sp):

            def load_x(t):
                if t.real:
                    wait_turn(sp, s_x1, 1, t.back(4), 1)
                    b = t.index * G
                    sp.dma_start(xs[:, t.slot(4)], x_by_node[:, bass.ds(b, G), :]).then_inc(s_x[t.slot(4)], 16)

            load_x(Turn(0, 0, UA, CHUNKS))
            sp.dma_start(adj_s[:], adj).then_inc(s_small, 16)
            sp.dma_start(eb[:, 0, :], edge_bias).then_inc(s_small, 16)
            sp.dma_start(eb[:, 1, :], out_edge_bias).then_inc(s_small, 16)
            for k, w in enumerate((gate_weight, out_gate_weight, loop_gate)):
                sp.dma_start(gate_w[:, k:k + 1], w).then_inc(s_small, 16)
            sp.dma_start(gate_b[:, 0:1], bias_gate).then_inc(s_small, 16)
            sp.dma_start(gate_b[:, 1:2], out_bias_gate).then_inc(s_small, 16)
            sp.dma_start(wg_s[:], Wg).then_inc(s_small, 16)
            sp.dma_start(bg_s[:], bg.partition_broadcast(P)).then_inc(s_small, 16)
            for k in range(1, UA):
                load_x(Turn(0, k, UA, CHUNKS))
            sp.dma_start(b1_s[:], b1).then_inc(s_bias, 16)
            sp.dma_start(b2_s[:], b2).then_inc(s_bias, 16)

            def w_source(k):
                layer, e = k // (E // 2), 2 * (k % (E // 2))
                if layer == 0:
                    return W1[e:e + 2].rearrange("e p h -> p e h")
                return W2[e:e + 2].rearrange("e (c p) d -> p e c d", p=P)

            def load_w(k):
                if k >= 2:
                    sp.wait_ge(s_wlo, k - 1)
                dst = w_in[:, k % 2]
                if k >= E // 2:
                    dst = dst.rearrange("p e (c d) -> p e c d", c=FC)
                src = w_source(k)
                for e in range(2):
                    sp.dma_start(dst[:, e], src[:, e]).then_inc(s_wl[k % 2], 16)

            def store_w(k):
                layer, e = k // (E // 2), 2 * (k % (E // 2))
                sp.wait_ge(s_wlo, k + 1)
                dst = w_dram[layer][e:e + 2].rearrange("e p h -> p e h")
                sp.dma_start(dst, w_split[:, k % 2].bitcast(F32).rearrange("p e k h -> p e (k h)")).then_inc(s_ws[k % 2], 16)

            load_w(0)
            load_w(1)

            sp.wait_ge(s_const, N_CONST)
            sp.dma_start(rows[0:1, :], zero_row[:]).then_inc(s_bs, 16)
            for k in range(E):
                store_w(k)
                if k + 2 < E:
                    load_w(k + 2)
                load_x(Turn(1 + k // UA, k % UA, UA, CHUNKS))
            for k in range(UA + E, CHUNKS):
                load_x(Turn(k // UA, k % UA, UA, CHUNKS))

            sp.wait_ge(s_texp, 1)
            sp.dma_start(experts_dram, code[0:NTG, :]).then_inc(s_tab, 16)
            sp.wait_ge(s_tab, 16)
            for i in range(2):
                sp.wait_ge(s_ws[i], 16 * E // 2)
            sp.wait_ge(s_bs, 16)

            def codes(t):
                both = sp.value_load(experts_dram[bass.ds(t.index, 1), :], min_val=0, max_val=16 * E + E)
                return [sp.snap(both >> 4, min_val=0, max_val=E), sp.snap(both & 15, min_val=0, max_val=E)]

            def load_slot(l, s, new, t, used, each):
                with sp.If_ne(sp.to_reg(new[s]), E):
                    wait_turn(sp, used[s], each, t, 0)
                    sp.dma_start(wt[l][:, s, :].bitcast(F32), w_dram[l][bass.ds(new[s], 1)].rearrange("a p h -> (a p) h")).then_inc(s_wt[l][s], 16)
                with sp.Else():
                    wait_turn(sp, used[s], each, t, 0)
                    sp.sem_inc(s_wt[l][s], 16)

            ahead = []

            def weights(t):
                new = ahead.pop() if t.step % UT else codes(t)
                load_slot(0, 0, new, t, s_mm1, 2)
                load_slot(0, 1, new, t, s_mm1, 2)
                load_slot(1, 0, new, t, s_mm2, 1)
                if t.step % UT < UT - 1:
                    ahead.append(codes(Turn(t.group, t.step + 1, UT, NT)))
                load_slot(1, 1, new, t, s_mm2, 1)

            every_turn(sp, UT, NT, weights)
            for i in range(UT):
                sp.wait_ge(s_out[i], 16 * BLK * ((NT + UT - 1 - i) // UT))

        @block.gpsimd
        def _(pool):
            own = Own(pool, s_pool)
            pool.memset(ones_f[:], 1.0).then_inc(s_const, 1)
            pool.memset(ident[:], 0.0).then_inc(s_const, 1)
            pool.memset(ones_b[:], 1.0).then_inc(s_const, 1)
            pool.memset(zeros_b[:], 0.0).then_inc(s_const, 1)
            pool.memset(keep[:], 1.0).then_inc(s_const, 1)
            pool.memset(step_e[:, 0, :], 0.0).then_inc(s_const, 1)
            pool.memset(step_e[:, 1, :], 1.0).then_inc(s_const, 1)
            pool.memset(zero_row[:], 0.0).then_inc(s_const, 1)
            pool.iota(iota_i[:], pattern=[[1, 256]], base=0, channel_multiplier=0).then_inc(s_const, 1)
            pool.iota(node_i[:], pattern=[[0, 1]], base=0, channel_multiplier=1).then_inc(s_const, 1)
            pool.wait_ge(s_const, 10)
            pool.affine_select(out=ident[:], in_=ident[:], pattern=[[-1, P]], compare_op=ALU.not_equal,
                               fill=1.0, base=0, channel_multiplier=1).then_inc(s_const, 1)
            pool.affine_select(out=before[:], in_=ones_b[:], pattern=[[1, P]], compare_op=ALU.is_gt,
                               fill=0.0, base=0, channel_multiplier=-1).then_inc(s_const, 1)
            pool.memset(keep[:, :, 0:1], 0.0).then_inc(s_const, 1)
            for c in range(1, NCLASS):
                for s in range(2):
                    d = FIRST[c][s] - FIRST[c - 1][s]
                    if d != s:
                        own(pool.memset(step_e[:, s, c:c + 1], float(d)))
            own.sync()
            pool.memset(row[:, :, :, 2 * P + 2:ROW], 0.0).then_inc(s_const, 1)

            def loop_message(t):
                if t.real:
                    wait_turn(pool, s_sig, 1, t, 1)
                    wait_turn(pool, s_tout, 2, t, 0)
                    gate = sig[:, t.slot(2), 2, :].unsqueeze(2).to_broadcast([P, G, D])
                    pool.tensor_tensor(t_loop, hs[:, t.slot(2)], gate, ALU.mult).then_inc(s_tloop, 1)

            def norm2(t, turn_):
                if t.real:
                    wait_turn(pool, s_norms, 1, turn_, 0)
                    r, rest = t.slot(4), G - BY_ACT
                    wide = lambda a: a[:, 1, BY_ACT:G].unsqueeze(2).to_broadcast([P, rest, D])
                    own(pool.tensor_tensor(row[:, r, BY_ACT:G, 0:P], row[:, r, BY_ACT:G, P:2 * P], wide(rstd), ALU.mult))
                    own.sync()
                    pool.tensor_tensor(row[:, r, BY_ACT:G, 0:P], row[:, r, BY_ACT:G, 0:P], wide(shift), ALU.add).then_inc(s_h2b, 1)

            def add_in(t):
                if t.real:
                    for k in range(2):
                        wait_turn(pool, s_tin, 2, t, k + 1)
                        wait_turn(pool, s_tout, 2, t, k + 1)
                        gs = slice(4 * k, 4 * k + 4)
                        last = pool.tensor_tensor(t_sum[:, gs], t_sum[:, gs], t_in[:, gs], ALU.add)
                    last.then_inc(s_tsum, 1)

            def split_lo(k):
                pool.wait_ge(s_whi, k + 1)
                if k >= 2:
                    pool.wait_ge(s_ws[k % 2], 16 * (k // 2))
                for e in range(2):
                    last = pool.tensor_tensor(w_split[:, k % 2, e, 1], w_in[:, k % 2, e],
                                              w_split[:, k % 2, e, 0].bitcast(F32), ALU.subtract)
                last.then_inc(s_wlo, 1)

            def turn(t):
                loop_message(t.back(2))
                norm2(t.back(4), t)
                add_in(t.back(2))
                for k in weight_steps(t):
                    split_lo(k)

            every_turn(pool, UA, CHUNKS, turn, own=own, **GRAPH_LOOP)

            def differences(t):
                wait_turn(pool, s_place, 1, Turn(t.group, 0, 1, 0), 1)
                wait_turn(pool, s_hot_n, 1, t, 1 - HOTS)
                pool.tensor_tensor(row_diff[:, t.slot(HOTS)], iota_b[:, 0:P].unsqueeze(1).to_broadcast([P, G, P]),
                                   row_at[:, bass.ds(t.index * G, G)].unsqueeze(2).to_broadcast([P, G, P]),
                                   ALU.subtract).then_inc(s_diff, 1)

            pool.wait_ge(s_iota, 6)
            every_turn(pool, HOTS, CHUNKS, differences)

            pool.wait_ge(s_index, 1)
            pool.wait_ge(s_btab, 1)
            pool.wait_ge(s_bs, 16)
            for i in range(4):
                pool.wait_ge(s_row[i], 16 * CHUNKS // 4)

            def gather(t, copied):
                s = t.slot(UT)
                wait_slot(pool, s_done, 1, t.back(UT), 1)
                wait_slot(pool, s_got, 16 * BLK, t, 0)
                pool.tensor_copy(from_row[:, s, :], index[:, bass.ds(t.index, 1), 0:BLK].rearrange("p a k -> p (a k)")).then_inc(copied, 1)
                pool.tensor_copy(b_t[:, s], b_of_tile[:, :, :, bass.ds(t.index, 1)].rearrange("p c s a -> p c (s a)")).then_inc(s_bt[s], 1)
                apart(pool, s_const)
                if copied is s_first:
                    pool.wait_ge(s_first, t.index + 1)
                else:
                    wait_slot(pool, s_from, 1, t.back(UT), 1)
                for j in range(BLK):
                    pool.indirect_dma_start(out=got[:, s, j, :], out_offset=None, in_=rows,
                                            in_offset=bass.IndirectOffsetOnAxis(ap=from_row[:, s, j:j + 1], axis=0)).then_inc(s_got[s], 16)

            def scatter(t):
                s = t.slot(UT)
                wait_slot(pool, s_done, 1, t, 1)
                wait_slot(pool, s_out, 16 * BLK, t, 0)
                pool.tensor_copy(to_row[:, s, :], index[:, bass.ds(t.index, 1), BLK:2 * BLK].rearrange("p a k -> p (a k)")).then_inc(s_to[s], 1)
                apart(pool, s_const)
                wait_slot(pool, s_to, 1, t, 1)
                for j in range(BLK):
                    pool.indirect_dma_start(out=out_rows, out_offset=bass.IndirectOffsetOnAxis(ap=to_row[:, s, j:j + 1], axis=0),
                                            in_=y_out[:, s, j, :], in_offset=None, bounds_check=TOKENS - 1,
                                            oob_is_err=False).then_inc(s_out[s], 16)

            def move(t):
                gather(Turn(t.group, t.step + UT, UT, NT), s_from[t.slot(UT)])
                scatter(t)

            for k in range(UT):
                gather(Turn(0, k, UT, NT), s_first)
            every_turn(pool, UT, NT, move, NTG - UT)
            for t in range(NTG - UT, NT):
                scatter(Turn(t // UT, t % UT, UT, NT))

        @block.scalar
        def _(act):
            def split_hi(k):
                act.wait_ge(s_wl[k % 2], 32 * (k // 2 + 1))
                if k >= 2:
                    act.wait_ge(s_ws[k % 2], 16 * (k // 2))
                for e in range(2):
                    last = act.activation(w_split[:, k % 2, e, 0], w_in[:, k % 2, e], ACT.Copy)
                last.then_inc(s_whi, 1)

            def gates(t):
                if t.real:
                    wait_turn(act, s_gate, 1, t, 1)
                    wait_turn(act, s_tout, 2, t, -2)
                    wait_turn(act, s_tloop, 1, t, -1)
                    for k in range(3):
                        bias = gate_b[:, k:k + 1] if k < 2 else 0.0
                        last = act.activation(sig[:, t.slot(2), k, :], ps_gate[:, :, k], ACT.Sigmoid, bias=bias)
                    last.then_inc(s_sig, 1)

            def times_in(t, halves):
                if t.real:
                    wait_turn(act, s_sig, 1, t, 1)
                    wait_turn(act, s_tsum, 1, t, 0)
                    for k in halves:
                        wait_turn(act, s_prod, 2, t, k + 1)
                        for b in range(4 * k, 4 * k + 4):
                            last = act.activation(t_in[:, b, :], ps_in[:, k, b % 4, :], ACT.Copy, scale=sig[:, t.slot(2), 0, b:b + 1])
                        last.then_inc(s_tin, 1)

            def norm1(t, turn_):
                if t.real:
                    wait_turn(act, s_norms, 1, turn_, 0)
                    wait_turn(act, s_prod, 2, t, -2)
                    wait_turn(act, s_tloop, 1, t, -1)
                    for b in range(G):
                        last = act.activation(hs[:, t.slot(2), b, :], xs[:, t.slot(4), b, :], ACT.Identity,
                                              scale=rstd[:, 0, b:b + 1], bias=shift[:, 0, b:b + 1])
                    last.then_inc(s_h, 1)

            def norm2(t, turn_):
                if t.real:
                    wait_turn(act, s_norms, 1, turn_, 0)
                    for b in range(BY_ACT):
                        last = act.activation(row[:, t.slot(4), b, 0:P], row[:, t.slot(4), b, P:2 * P], ACT.Identity,
                                              scale=rstd[:, 1, b:b + 1], bias=shift[:, 1, b:b + 1])
                    last.then_inc(s_h2, 1)

            def copy_t(t, s_from, s_done_, dst, s_free):
                if t.real:
                    wait_turn(act, s_free, 1, t, 0)
                    for k in range(2):
                        wait_turn(act, s_from, 2, t, k + 1)
                        act.activation(dst[:, 4 * k:4 * k + 4, :], ps_t[:, k], ACT.Copy).then_inc(s_done_, 1)

            def row_weights(t):
                if t.real:
                    wait_turn(act, s_margin, 1, t, 1)
                    act.activation(row[:, t.slot(4), :, 2 * P], margin[:], ACT.Sigmoid)
                    act.activation(row[:, t.slot(4), :, 2 * P + 1], margin[:], ACT.Sigmoid, scale=-1.0).then_inc(s_rw, 1)

            def store_row(t):
                if t.real:
                    wait_turn(act, s_rw, 1, t, 1)
                    b = t.index * G
                    act.dma_start(rows_by_node[:, bass.ds(b, G), :], row[:, t.slot(4)]).then_inc(s_row[t.slot(4)], 16)

            def turn(t):
                norm1(t.back(1), t)
                row_weights(t.back(6))
                norm2(t.back(4), t)
                store_row(t.back(6))
                times_in(t.back(2), [0])
                copy_t(t.back(1), s_ht_ps, s_ht, hT, s_gate)
                times_in(t.back(2), [1])
                copy_t(t.back(4), s_h2t_ps, s_h2t, h2T, s_logit)
                gates(t.back(1))
                for k in weight_steps(t):
                    split_hi(k)

            act.wait_ge(s_small, 16 * 10)
            act.wait_ge(s_const, N_CONST)
            act.activation(ident_r[:], ident[:], ACT.Copy).then_inc(s_adj, 1)
            every_turn(act, UA, CHUNKS, turn, **GRAPH_LOOP)

            def times_graph(t):
                s = t.slot(HOTS)
                wait_turn(act, s_hot, 1, t, 1)
                wait_turn(act, s_inv, 1, t, 1 - HOTS)
                for b in range(G):
                    last = act.activation(at_row_b[:, s, b], at_row[:, s, b], ACT.Copy, scale=graph_f[:, bass.ds(t.index * G + b, 1)])
                last.then_inc(s_hot_b, 1)

            act.wait_ge(s_iota, 6)
            every_turn(act, HOTS, CHUNKS, times_graph)

            act.wait_ge(s_b_ps, 1)
            act.activation(b_of_tile[:], ps_bias, ACT.Copy).then_inc(s_btab, 1)

            def tile_hi(t):
                wait_turn(act, s_xt, 1, t, 1)
                wait_turn(act, s_mm1[1], 2, t, -2)
                act.activation(in_hi[:, t.slot(2)], ps_x, ACT.Copy).then_inc(s_inhi, 1)

            def gelu(t, s):
                wait_turn(act, s_split[s], 2, t, 0)
                if s == 0:
                    wait_slot(act, s_bt, 1, t, 1)
                for c in range(FC):
                    if c % 2 == 0:
                        wait_turn(act, s_mm1[s], 2, t, c // 2 + 1)
                    act.activation(act_f[:, s, c, :], ps_h[s][:, c, :], ACT.Gelu, bias=b_t[:, t.slot(UT), c, s:s + 1]).then_inc(s_act[s], 1)

            def copy_y(t, s):
                if t.real:
                    wait_turn(act, s_mm2[s], 1, t, 1)
                    wait_turn(act, s_o, 1, t, 0)
                    act.activation(y_t[:, s, :], ps_y[s], ACT.Identity, bias=b_t[:, t.slot(UT), FC, s:s + 1]).then_inc(s_y[s], 1)

            def tile(t):
                gelu(t, 0)
                copy_y(t.back(1), 1)
                tile_hi(Turn(t.group, t.step + 1, UT, NT))
                gelu(t, 1)
                copy_y(t, 0)

            tile_hi(Turn(0, 0, UT, NT))
            every_turn(act, UT, NT, tile)
            copy_y(END.back(1), 1)

        @block.vector
        def _(dve):
            own = Own(dve, s_dve)

            dve.wait_ge(s_const, N_CONST)
            dve.tensor_copy(iota_f[:], iota_i[:]).then_inc(s_iota, 1)
            dve.tensor_copy(iota_b[:], iota_i[:]).then_inc(s_iota, 1)
            dve.tensor_scalar(graph_f[:], iota_i[:, 0:NB], 1.0, None, ALU.add).then_inc(s_iota, 1)
            dve.tensor_copy(node_f[:], node_i[:]).then_inc(s_iota, 1)
            dve.tensor_scalar(node_b[:, 0:1], node_i[:], -1.0, None, ALU.add).then_inc(s_iota, 1)
            dve.tensor_scalar(node_b[:, 1:2], node_i[:], 0.0, None, ALU.is_equal).then_inc(s_iota, 1)

            def matrices():
                dve.wait_ge(s_small, 16 * 10)
                dve.wait_ge(s_adjt, 1)
                own(dve.tensor_copy(adj_t[:], ps_t[:, 0, 0, :]))
                own(dve.scalar_tensor_tensor(out=tmp_m[:, 1, :], in0=adj_s[:], scalar=0.0, in1=adj_s[:], op0=ALU.is_le, op1=ALU.mult))
                own.sync()
                own(dve.scalar_tensor_tensor(out=tmp_m[:, 0, :], in0=adj_t[:], scalar=0.0, in1=adj_t[:], op0=ALU.is_le, op1=ALU.mult))
                own.sync()
                own(dve.scalar_tensor_tensor(out=adj_out[:], in0=adj_s[:], scalar=0.0, in1=tmp_m[:, 1, :], op0=ALU.is_gt, op1=ALU.add))
                own(dve.scalar_tensor_tensor(out=adj_in[:], in0=adj_t[:], scalar=0.0, in1=tmp_m[:, 0, :], op0=ALU.is_gt, op1=ALU.add))
                own.sync()
                own(dve.tensor_tensor(tmp_m[:, 0, :], adj_in[:], adj_t[:], ALU.mult))
                own(dve.tensor_tensor(tmp_m[:, 1, :], adj_out[:], adj_t[:], ALU.mult))
                own.sync()
                dve.tensor_copy(adj_in[:], tmp_m[:, 0, :]).then_inc(s_adj, 1)
                dve.tensor_copy(adj_out[:], tmp_m[:, 1, :]).then_inc(s_adj, 1)
                for k in range(2):
                    src = eb[:, k, :].unsqueeze(1).to_broadcast([P, 4, P])
                    own(dve.tensor_copy(eb_hi[:, k], src))
                    own.sync()
                    dve.tensor_tensor(eb_lo[:, k], src, eb_hi[:, k].bitcast(F32), ALU.subtract).then_inc(s_adj, 1)

            def turn(t):
                one, mid, two, rt_ = t, t.back(2), t.back(3), t.back(5)
                norms = one.real or two.real

                if one.real:
                    wait_slot(dve, s_x, 16, one, 16)
                    for b in range(G):
                        own(dve.bn_stats(stats[:, 0, b, :], xs[:, one.slot(4), b, :]))
                if two.real:
                    wait_turn(dve, s_tsum, 1, two, 1)
                    wait_slot(dve, s_row, 16, two, 0)
                    dve.scalar_tensor_tensor(out=row[:, two.slot(4), :, P:2 * P], in0=t_sum, scalar=0.0,
                                             in1=xs[:, two.slot(4)], op0=ALU.max, op1=ALU.add).then_inc(s_x1, 1)
                if rt_.real:
                    wait_turn(dve, s_logit, 1, rt_, 1)
                    dve.tensor_tensor(logit[:], ps_logit, bg_s[:].unsqueeze(1).to_broadcast([P, G, E]), ALU.add).then_inc(s_lsum, 1)
                if two.real:
                    wait_turn(dve, s_x1, 1, two, 1)
                    for b in range(G):
                        own(dve.bn_stats(stats[:, 1, b, :], row[:, two.slot(4), b, P:2 * P]))
                if mid.real:
                    wait_turn(dve, s_tloop, 1, mid, 1)
                    wait_turn(dve, s_x1, 1, mid, 0)

                def times_out(b):
                    if mid.real:
                        if b % 4 == 0:
                            wait_turn(dve, s_prod, 2, mid, b // 4 + 1)
                        ins = dve.scalar_tensor_tensor(out=t_sum[:, b, :], in0=ps_out[:, b // 4, b % 4, :],
                                                       scalar=sig[:, mid.slot(2), 1, b:b + 1], in1=t_loop[:, b, :],
                                                       op0=ALU.mult, op1=ALU.add)
                        if b % 4 == 3:
                            ins.then_inc(s_tout, 1)

                msum, mdiff, m2, dd, var, y, a, c = (ln_tmp[:, i] for i in range(8))
                low, high, order, sign, diff, half, prod, class_ = (rt[:, i, :] for i in range(8))
                if rt_.real:
                    b0 = rt_.index * G
                    wait_turn(dve, s_lsum, 1, rt_, 1)
                own.sync()
                if norms:
                    st = stats[:]
                    own(dve.tensor_tensor(msum, st[:, :, :, 1], st[:, :, :, 4], ALU.add))
                    own(dve.tensor_tensor(mdiff, st[:, :, :, 1], st[:, :, :, 4], ALU.subtract))
                    own(dve.tensor_tensor(m2, st[:, :, :, 2], st[:, :, :, 5], ALU.add))
                if rt_.real:
                    for b in range(G):
                        own(dve.max(top[:, b, :], logit[:, b, :]))
                own.sync()
                if norms:
                    own(dve.tensor_tensor(dd, mdiff, mdiff, ALU.mult))
                if rt_.real:
                    own(dve.tensor_tensor(diff, top[:, :, 0], top[:, :, 1], ALU.subtract))
                    for b in range(G):
                        own(dve.max_index(top_at[:, b, :], top[:, b, :], logit[:, b, :]))
                own.sync()
                if norms:
                    own(dve.scalar_tensor_tensor(out=a, in0=dd, scalar=D / 4.0, in1=m2, op0=ALU.mult, op1=ALU.add))
                if rt_.real:
                    i0, i1 = top_at[:, :, 0], top_at[:, :, 1]
                    own(dve.tensor_tensor(low, i0, i1, ALU.min))
                    own(dve.tensor_tensor(high, i0, i1, ALU.max))
                    own(dve.tensor_tensor(order, i0, i1, ALU.is_lt))
                own.sync()
                if norms:
                    own(dve.tensor_scalar(var, a, 1.0 / D, EPS, ALU.mult, ALU.add))
                if rt_.real:
                    own(dve.tensor_scalar(sign, order, 2.0, -1.0, ALU.mult, ALU.add))
                    own(dve.tensor_scalar(half, low, -0.5, E - 1.5, ALU.mult, ALU.add))
                times_out(0)
                own.sync()
                if norms:
                    own(dve.tensor_scalar(ln_bits[:, 0], var.bitcast(I32), 1, None, ALU.logical_shift_right))
                if rt_.real:
                    wait_turn(dve, s_rw, 1, rt_, 0)
                    dve.tensor_tensor(margin[:], diff, sign, ALU.mult).then_inc(s_margin, 1)
                    own(dve.tensor_tensor(prod, half, low, ALU.mult))
                own.sync()
                if norms:
                    own(dve.tensor_scalar(ln_bits[:, 1], ln_bits[:, 0], -1.0, RSQRT_SEED, ALU.mult, ALU.add))
                if rt_.real:
                    own(dve.scalar_tensor_tensor(out=class_, in0=prod, scalar=-1.0, in1=high, op0=ALU.add, op1=ALU.add))
                times_out(1)
                own.sync()
                now = ln_bits[:, 1].bitcast(F32)
                if norms:
                    own(dve.tensor_tensor(a, now, now, ALU.mult))
                if rt_.real:
                    own(dve.tensor_copy(class_of[:, bass.ds(b0, G)], class_))
                    own(dve.tensor_copy(hot[:, :, 0:1], count[:, :, G:G + 1]))
                    own(dve.tensor_tensor(hot[:, :, 1:G + 1], iota_f[:, 0:NCLASS].unsqueeze(2).to_broadcast([P, NCLASS, G]),
                                          class_.unsqueeze(1).to_broadcast([P, NCLASS, G]), ALU.is_equal))
                own.sync()
                if norms:
                    own(dve.scalar_tensor_tensor(out=c, in0=a, scalar=-0.5, in1=var, op0=ALU.mult, op1=ALU.mult))
                if rt_.real:
                    own(dve.tensor_tensor_scan(count[:].rearrange("p c g -> p (c g)"), keep[:].rearrange("p c g -> p (c g)"),
                                               hot[:].rearrange("p c g -> p (c g)"), 0.0, ALU.mult, ALU.add))
                own.sync()
                if norms:
                    own(dve.scalar_tensor_tensor(out=y, in0=c, scalar=1.5, in1=now, op0=ALU.add, op1=ALU.mult))
                if rt_.real:
                    own(dve.tensor_tensor(ranked[:], hot[:, :, 1:G + 1], count[:, :, 0:G], ALU.mult))
                own.sync()
                if norms:
                    own(dve.tensor_tensor(a, y, y, ALU.mult))
                if rt_.real:
                    own(dve.tensor_reduce(rank_of[:, bass.ds(b0, G)], ranked[:].rearrange("p c g -> p g c"), AX_X, ALU.add))
                times_out(2)
                own.sync()
                if norms:
                    own(dve.scalar_tensor_tensor(out=c, in0=a, scalar=-0.5, in1=var, op0=ALU.mult, op1=ALU.mult))
                times_out(3)
                own.sync()
                if norms:
                    own(dve.scalar_tensor_tensor(out=dd, in0=c, scalar=1.5, in1=y, op0=ALU.add, op1=ALU.mult))
                times_out(4)
                own.sync()
                if norms:
                    own(dve.tensor_tensor(a, dd, dd, ALU.mult))
                times_out(5)
                own.sync()
                if norms:
                    own(dve.scalar_tensor_tensor(out=c, in0=a, scalar=-0.5, in1=var, op0=ALU.mult, op1=ALU.mult))
                times_out(6)
                own.sync()
                if norms:
                    if one.real:
                        wait_turn(dve, s_h, 1, one, 0)
                    else:
                        dve.wait_ge(s_h, CHUNKS)
                    wait_turn(dve, s_h2, 1, two, 0)
                    wait_turn(dve, s_h2b, 1, two, 0)
                    own(dve.scalar_tensor_tensor(out=rstd[:], in0=c, scalar=1.5, in1=dd, op0=ALU.add, op1=ALU.mult))
                times_out(7)
                own.sync()
                if norms:
                    dve.scalar_tensor_tensor(out=shift[:], in0=msum, scalar=-0.5, in1=rstd[:],
                                             op0=ALU.mult, op1=ALU.mult).then_inc(s_norms, 1)
                if isinstance(t.index, int) and t.index == 0:
                    matrices()

            own(dve.memset(count[:], 0.0))
            own(dve.memset(stats[:], 1.0))
            own.sync()
            every_turn(dve, UA, CHUNKS, turn, own=own, **GRAPH_LOOP)

            own.sync()
            dve.tensor_copy(totals[:], count[:, :, G]).then_inc(s_tot, 1)
            dve.wait_ge(s_tot_ps, 1)
            tiles_f, upto, base, offset, ones_c = (pl[:, i, :] for i in range(5))
            own(dve.tensor_scalar(pl_i[:, 0, :], ps_tot, TILE - 1.0, None, ALU.add))
            own(dve.memset(ones_c, 1.0))
            own.sync()
            own(dve.tensor_scalar(pl_i[:, 1, :], pl_i[:, 0, :], TILE.bit_length() - 1, None, ALU.logical_shift_right))
            own.sync()
            own(dve.tensor_copy(tiles_f, pl_i[:, 1, :]))
            own.sync()
            own(dve.tensor_tensor_scan(upto, ones_c, tiles_f, 0.0, ALU.mult, ALU.add))
            own.sync()
            own(dve.tensor_tensor(base, upto, tiles_f, ALU.subtract))
            own.sync()
            own(dve.scalar_tensor_tensor(out=offset, in0=base, scalar=float(TILE), in1=ps_pre, op0=ALU.mult, op1=ALU.add))
            own(dve.tensor_scalar(started[:, 0, :], base, node_f[:], None, ALU.is_le))
            own(dve.tensor_scalar(started[:, 1, :], base, node_b[:, 0:1], None, ALU.is_le))
            own.sync()
            for k in range(2):
                for s in range(2):
                    own(dve.tensor_tensor(steps[:, 2 * k + s, :], started[:, k, :], step_e[:, s, :], ALU.mult))
            own.sync()
            own(dve.tensor_reduce(expert[:], steps[:], AX_X, ALU.add))
            own.sync()
            dve.tensor_copy(expert_rep[:], expert[:, 0:2].unsqueeze(2).to_broadcast([P, 2, E])).then_inc(s_rep, 1)
            own(dve.tensor_tensor(change[:, 0, :], expert[:, 0:2], expert[:, 2:4], ALU.subtract))
            own.sync()
            own(dve.tensor_tensor(change[:, 1, :], change[:, 0, :], change[:, 0, :], ALU.mult))
            own.sync()
            own(dve.tensor_scalar(change[:, 2, :], change[:, 1, :], node_b[:, 1:2], 0.0, ALU.add, ALU.is_gt))
            own.sync()
            own(dve.scalar_tensor_tensor(out=change[:, 0, :], in0=expert[:, 0:2], scalar=-float(E), in1=change[:, 2, :], op0=ALU.add, op1=ALU.mult))
            own.sync()
            own(dve.tensor_scalar(change[:, 1, :], change[:, 0, :], float(E), None, ALU.add))
            own.sync()
            dve.scalar_tensor_tensor(out=code[:], in0=change[:, 1, 0:1], scalar=16.0, in1=change[:, 1, 1:2],
                                     op0=ALU.mult, op1=ALU.add).then_inc(s_texp, 1)
            dve.wait_ge(s_exp_ps, 1)
            dve.tensor_scalar(expert_hot[:], ps_exp, node_f[0:E, :], None, ALU.is_equal).then_inc(s_exp_hot, 1)

            def places(group):
                b0 = group * PIECE
                own(dve.tensor_tensor(pick[:, 0], iota_f[:, 0:NCLASS].unsqueeze(1).to_broadcast([P, PIECE, NCLASS]),
                                      class_of[:, bass.ds(b0, PIECE)].unsqueeze(2).to_broadcast([P, PIECE, NCLASS]), ALU.is_equal))
                own.sync()
                own(dve.tensor_tensor(pick[:, 1], pick[:, 0], offset.unsqueeze(1).to_broadcast([P, PIECE, NCLASS]), ALU.mult))
                own.sync()
                own(dve.tensor_reduce(place[:], pick[:, 1], AX_X, ALU.add))
                own.sync()
                own(dve.tensor_tensor(place_i[:], place[:], rank_of[:, bass.ds(b0, PIECE)], ALU.add))
                own.sync()
                own(dve.tensor_scalar(place_at[:], place_i[:], P - 1, None, ALU.bitwise_and))
                own.sync()
                own(dve.tensor_copy(row_at[:, bass.ds(b0, PIECE)], place_at[:]))
                own(dve.tensor_scalar(col_at[:, bass.ds(b0, PIECE)], place_i[:], P.bit_length() - 1, None, ALU.logical_shift_right))
                own.sync()
                dve.sem_inc(s_place, 1)

            def hots(t):
                s, b0 = t.slot(HOTS), t.index * G
                wait_turn(dve, s_inv, 1, t, 1 - HOTS)
                wait_turn(dve, s_hot_b, 1, t, 1 - HOTS)
                wait_turn(dve, s_diff, 1, t, 1)
                dve.tensor_scalar(at_row[:, s], row_diff[:, s], 0.0, None, ALU.is_equal).then_inc(s_hot, 1)
                dve.tensor_scalar(at_row_n[:, s], row_diff[:, s], 0.0, node_f[:], ALU.is_equal, ALU.mult).then_inc(s_hot_n, 1)
                dve.tensor_tensor(at_col[:, s], iota_b[:, 0:COLS].unsqueeze(1).to_broadcast([P, G, COLS]),
                                  col_at[:, bass.ds(b0, G)].unsqueeze(2).to_broadcast([P, G, COLS]), ALU.is_equal).then_inc(s_hot_c, 1)

            def piece(t):
                for k in range(HOTS):
                    hots(Turn(t.index, k, HOTS, CHUNKS))
                    if k == 0 and t.real and Turn(t.group, t.step + 1, 1, t.total).real:
                        places(t.index + 1)

            places(0)
            every_turn(dve, 1, NB // PIECE, piece, last=NB // PIECE - 1, own=own)

            dve.wait_ge(s_inv, CHUNKS + 1)
            node, graph, empty, target = (inv[:, i, :] for i in range(4))
            own(dve.tensor_copy(node, ps_a))
            own(dve.tensor_copy(graph, ps_b))
            own.sync()
            shaped = lambda a: a.rearrange("p (t j) -> p t j", j=BLK)
            own(dve.scalar_tensor_tensor(out=index[:, :, 0:BLK], in0=shaped(node), scalar=float(NB), in1=shaped(graph), op0=ALU.mult, op1=ALU.add))
            own(dve.tensor_scalar(empty, graph, 0.0, 4.0 * TOKENS, ALU.is_equal, ALU.mult))
            own(dve.scalar_tensor_tensor(out=target, in0=graph, scalar=float(N), in1=node, op0=ALU.mult, op1=ALU.add))
            own.sync()
            dve.scalar_tensor_tensor(out=index[:, :, BLK:2 * BLK], in0=shaped(target), scalar=-float(N), in1=shaped(empty),
                                     op0=ALU.add, op1=ALU.add).then_inc(s_index, 1)

            def tile_lo(t):
                wait_turn(dve, s_inhi, 1, t, 1)
                k = t.slot(2)
                dve.tensor_tensor(in_lo[:, k], ps_x, in_hi[:, k].bitcast(F32), ALU.subtract).then_inc(s_inlo, 1)

            def split(t, s):
                wait_turn(dve, s_mm2[s], 1, t, 0)
                for k in range(2):
                    cs = slice(k * FC // 2, (k + 1) * FC // 2)
                    wait_turn(dve, s_act[s], FC, t, (k + 1) * FC // 2)
                    dve.tensor_copy(act_hi[:, s, cs, :], act_f[:, s, cs, :]).then_inc(s_hhi, 1)
                    wait_turn(dve, s_hhi, 4, t, 2 * s + k + 1)
                    dve.tensor_tensor(act_lo[:, s, cs, :], act_f[:, s, cs, :], act_hi[:, s, cs, :].bitcast(F32),
                                      ALU.subtract).then_inc(s_split[s], 1)

            def sum_up(t):
                if t.real:
                    i = t.slot(UT)
                    wait_turn(dve, s_o, 1, t, 1)
                    for j in range(BLK):
                        last = dve.scalar_tensor_tensor(out=y_one[:, j, :], in0=ps_o[:, 0, j, :], scalar=got[:, i, j, 2 * P:2 * P + 1],
                                                        in1=got[:, i, j, P:2 * P], op0=ALU.mult, op1=ALU.add)
                    last.then_inc(s_y1, 1)
                    wait_turn(dve, s_y1, 1, t, 1)
                    wait_slot(dve, s_out, 16 * BLK, t, 0)
                    for j in range(BLK):
                        last = dve.scalar_tensor_tensor(out=y_out[:, i, j, :], in0=ps_o[:, 1, j, :], scalar=got[:, i, j, 2 * P + 1:2 * P + 2],
                                                        in1=y_one[:, j, :], op0=ALU.mult, op1=ALU.add)
                    last.then_inc(s_done[i], 1)

            def tile(t):
                split(t, 0)
                tile_lo(Turn(t.group, t.step + 1, UT, NT))
                split(t, 1)
                sum_up(t.back(1))

            tile_lo(Turn(0, 0, UT, NT))
            every_turn(dve, UT, NT, tile)
            sum_up(END.back(1))

        @block.tensor
        def _(pe):
            pe.wait_ge(s_const, N_CONST)
            pe.wait_ge(s_small, 16 * 10)
            pe.transpose(ps_t[:, 0, 0, :], adj_s[:], ident[:]).then_inc(s_adjt, 1)
            pe.wait_ge(s_adj, 5)

            def transposed(t, src, s_src, s_dst, bank_free, more):
                wait_turn(pe, s_src, 1, t, 1)
                if s_src is s_h2:
                    wait_turn(pe, s_h2b, 1, t, 1)
                for b in range(G):
                    if b % 4 == 0:
                        wait_turn(pe, *bank_free, more + b // 4)
                    last = pe.transpose(ps_t[:, b // 4, b % 4, :], src(b), ident[:])
                    if b % 4 == 3:
                        last.then_inc(s_dst, 1)

            def products(t, halves):
                if t.real:
                    wait_turn(pe, s_h, 1, t, 1)
                    for k in halves:
                        rhs = hs[:, t.slot(2), 4 * k:4 * k + 4, :]
                        wait_turn(pe, s_tin, 2, t, k - 1)
                        wait_turn(pe, s_tout, 2, t, k - 1)
                        for dst, w, e in ((ps_in, adj_in, 0), (ps_out, adj_out, 1)):
                            pe.matmul(dst[:, k], w[:], rhs, start=True, stop=False)
                            pe.matmul(dst[:, k], ident_r[:], eb_hi[:, e], start=False, stop=False)
                            last = pe.matmul(dst[:, k], ident_r[:], eb_lo[:, e], start=False, stop=True)
                        last.then_inc(s_prod, 1)

            def small(t, s_src, src, w, dst, s_free, s_dst):
                if t.real:
                    wait_turn(pe, s_src, 2, t, 2)
                    wait_turn(pe, s_free, 1, t, 0)
                    for b in range(G):
                        last = pe.matmul(dst(b), src[:, b, :], w[:], start=True, stop=True)
                    last.then_inc(s_dst, 1)

            def turn(t):
                one, two = t.back(1), t.back(4)
                products(t.back(2), [0])
                h2t_before = (s_h2t, 2, two)
                if one.real:
                    transposed(one, lambda b: hs[:, one.slot(2), b, :], s_h, s_ht_ps, h2t_before, -1)
                products(t.back(2), [1])
                if two.real:
                    transposed(two, lambda b: row[:, two.slot(4), b, 0:P], s_h2, s_h2t_ps,
                               *(((s_ht, 2, one), 1) if one.real else (h2t_before, -1)))
                small(one, s_ht, hT, gate_w, lambda b: ps_gate[:, b, 0:3], s_sig, s_gate)
                small(two, s_h2t, h2T, wg_s, lambda b: ps_logit[:, b, :], s_lsum, s_logit)

            every_turn(pe, UA, CHUNKS, turn, **GRAPH_LOOP)

            pe.wait_ge(s_tot, 1)
            pe.matmul(ps_pre, before[:], totals[:], start=True, stop=True)
            pe.matmul(ps_tot, ones_b[:], totals[:], start=True, stop=True).then_inc(s_tot_ps, 1)

            pe.wait_ge(s_rep, 1)
            pe.wait_ge(s_bias, 32)
            for s in range(2):
                last = pe.matmul(ps_exp[:, s, :], expert_rep[:, s, :], ident[:], start=True, stop=True)
            last.then_inc(s_exp_ps, 1)
            pe.wait_ge(s_exp_hot, 1)
            for c in range(FC):
                pe.matmul(ps_bias[:, c], b1_s[:, c * P:(c + 1) * P], expert_hot[:], start=True, stop=True)
            last = pe.matmul(ps_bias[:, FC], b2_s[:], expert_hot[:], start=True, stop=True)
            last.then_inc(s_b_ps, 1)

            def inverse(t):
                wait_turn(pe, s_hot_n, 1, t, 1)
                wait_turn(pe, s_hot_b, 1, t, 1)
                s = t.slot(HOTS)
                wait_turn(pe, s_hot_c, 1, t, 1)
                for b in range(G):
                    pe.matmul(ps_a, at_row_n[:, s, b, :], at_col[:, s, b, :], start=False, stop=False)
                    last = pe.matmul(ps_b, at_row_b[:, s, b, :], at_col[:, s, b, :], start=False, stop=False)
                last.then_inc(s_inv, 1)

            for dst in (ps_a, ps_b):
                pe.matmul(dst, zeros_b[:, 0:P], zeros_b[:], start=True, stop=False)
            every_turn(pe, HOTS, CHUNKS, inverse)
            for dst in (ps_a, ps_b):
                last = pe.matmul(dst, zeros_b[:, 0:P], zeros_b[:], start=False, stop=True)
            last.then_inc(s_inv, 1)

            pe.wait_ge(s_btab, 1)

            def tile_in(t):
                s = t.slot(UT)
                wait_slot(pe, s_got, 16 * BLK, t, 16 * BLK)
                wait_turn(pe, s_inlo, 1, t, 0)
                for j in range(BLK):
                    last = pe.transpose(ps_x[:, j * P:(j + 1) * P], got[:, s, j, 0:P], ident[:])
                last.then_inc(s_xt, 1)

            def layer1(t, s):
                k = t.slot(2)
                wait_turn(pe, s_wt[0][s], 16, t, 16)
                wait_turn(pe, s_inlo, 1, t, 1)
                wait_turn(pe, s_inhi, 1, t, 1)
                wait_turn(pe, s_act[s], FC, t, 0)
                for c in range(FC):
                    hi = wt[0][:, s, c * P:(c + 1) * P]
                    lo = wt[0][:, s, H + c * P:H + (c + 1) * P]
                    pe.matmul(ps_h[s][:, c, :], hi, in_hi[:, k], start=True, stop=False)
                    pe.matmul(ps_h[s][:, c, :], hi, in_lo[:, k], start=False, stop=False)
                    last = pe.matmul(ps_h[s][:, c, :], lo, in_hi[:, k], start=False, stop=True)
                    if c % 2:
                        last.then_inc(s_mm1[s], 1)

            def layer2(t, s):
                if t.real:
                    wait_turn(pe, s_wt[1][s], 16, t, 16)
                    wait_turn(pe, s_y[s], 1, t, 0)
                    for c in range(FC):
                        if c % 2 == 0:
                            wait_turn(pe, s_split[s], 2, t, c // 2 + 1)
                        hi = wt[1][:, s, c * P:(c + 1) * P]
                        lo = wt[1][:, s, H + c * P:H + (c + 1) * P]
                        pe.matmul(ps_y[s], hi, act_hi[:, s, c, :], start=(c == 0), stop=False)
                        pe.matmul(ps_y[s], hi, act_lo[:, s, c, :], start=False, stop=False)
                        last = pe.matmul(ps_y[s], lo, act_hi[:, s, c, :], start=False, stop=(c == FC - 1))
                    last.then_inc(s_mm2[s], 1)

            def tile_out(t):
                if t.real:
                    for s in range(2):
                        wait_turn(pe, s_y[s], 1, t, 1)
                    wait_slot(pe, s_done, 1, t.back(1), 1)
                    for s in range(2):
                        for j in range(BLK):
                            last = pe.transpose(ps_o[:, s, j, :], y_t[:, s, j * P:(j + 1) * P], ident[:])
                    last.then_inc(s_o, 1)

            def tile(t):
                layer1(t, 0)
                layer2(t.back(1), 1)
                tile_in(Turn(t.group, t.step + 1, UT, NT))
                layer1(t, 1)
                tile_out(t.back(1))
                layer2(t, 0)

            tile_in(Turn(0, 0, UT, NT))
            every_turn(pe, UT, NT, tile)
            layer2(END.back(1), 1)
            tile_out(END.back(1))


_INS = ["x", "adj", "L0_gnn_edge_bias", "L0_gnn_gate_weight", "L0_gnn_bias_gate", "L0_gnn_out_edge_bias",
        "L0_gnn_out_gate_weight", "L0_gnn_out_bias_gate", "L0_gnn_loop_gate", "L0_ffn_Wg", "L0_ffn_bg",
        "L0_ffn_W1", "L0_ffn_b1", "L0_ffn_W2", "L0_ffn_b2"]


def kernel(**inputs):
    import numpy as _np
    import concourse.bacc as _bacc
    from concourse import mybir as _mybir
    from concourse.bass_utils import run_bass_kernel_spmd as _run

    nc = _bacc.Bacc("TRN2", target_bir_lowering=False, num_devices=1)
    arrays, args = {}, []
    for name in _INS:
        a = _np.ascontiguousarray(inputs[name])
        arrays[f"in_{name}_dram"] = a
        args.append(nc.dram_tensor(f"in_{name}_dram", a.shape, _mybir.dt.from_np(a.dtype), kind="ExternalInput").ap())
    shape = inputs["x"].shape
    args.append(nc.dram_tensor("out_0_dram", shape, _mybir.dt.float32, kind="ExternalOutput").ap())
    program(nc, *args)
    r = _run(nc, [arrays], core_ids=[0])
    return r.results[0]["out_0_dram"]
```
